# Optimizing a Trainium2 kernel written in Bass

```python
import numpy as np
import jax
import jax.numpy as jnp

def _softmax(x, axis=-1):
    return jax.nn.softmax(x, axis=axis)

def _gelu(x):
    return jax.nn.gelu(x, approximate=True)

def _silu(x):
    return jax.nn.silu(x)

def _sigmoid(x):
    return jax.nn.sigmoid(x)

def _layernorm(x, axis=-1, eps=1e-05):
    m = jnp.mean(x, axis=axis, keepdims=True)
    v = jnp.var(x, axis=axis, keepdims=True)
    return (x - m) / jnp.sqrt(v + eps)

def _scatter_add(tgt, idx, src, axis=0):
    return tgt.at[idx].add(src)

def _segment_sum(src, seg, n):
    return jax.ops.segment_sum(src, seg, n)
kernel_name = 'mk_recurrent_d1_jaxref_r4_cc34ae'

def setup_inputs(seed: int=0):
    np.random.seed(seed)
    _w = jnp.asarray

    def _L0_attn_setup():
        import jax, jax.numpy as jnp
        import numpy as np
        B, T, HID = (4, 512, 256)
        NH = 4
        KD, VD = (128, 256)
        DK, DV = (KD // NH, VD // NH)
        R = 32
        GLR = 64
        EPS = 1e-05

        def _rwkv6_scan(r, k, v, w, u):

            def step(S, xs):
                r_t, k_t, v_t, w_t = xs
                kv = k_t[..., :, None] * v_t[..., None, :]
                o_t = jnp.einsum('bhk,bhkv->bhv', r_t, S + u[None, :, :, None] * kv)
                S = jnp.exp(w_t)[..., None] * S + kv
                return (S, o_t)
            S0 = jnp.zeros(r.shape[:2] + (r.shape[-1], v.shape[-1]), r.dtype)
            mv = lambda x: jnp.moveaxis(x, 2, 0)
            _, o = jax.lax.scan(step, S0, (mv(r), mv(k), mv(v), mv(w)))
            return jnp.moveaxis(o, 0, 2)
        key = jax.random.key(seed)
        ks = jax.random.split(key, 20)
        g = lambda i, shape, s=0.02: jax.random.normal(ks[i], shape, dtype=jnp.float32) * s
        return {'hidden_states': jax.random.normal(ks[0], (B, T, HID), dtype=jnp.float32), 'mu0': g(1, (HID,), 0.1), 'W_x0': g(2, (5 * R, HID)), 'W_x2': g(3, (HID, 5 * R)), 'x_bias': g(4, (5, HID), 0.1), 'W_r': g(5, (KD, HID)), 'W_w1': g(6, (GLR, HID)), 'W_w2': g(7, (KD, GLR)), 'b_w2': g(8, (KD,), 0.1), 'W_k': g(9, (KD, HID)), 'W_v': g(10, (VD, HID)), 'W_g': g(11, (VD, HID)), 'bonus': g(12, (NH, DK), 0.1), 'gn_weight': jnp.ones((VD,), jnp.float32) + g(13, (VD,), 0.05), 'gn_bias': g(14, (VD,), 0.05), 'W_o': g(15, (HID, VD))}
    _L0_attn_in = _L0_attn_setup()

    def _L0_ffn_setup():
        import jax, jax.numpy as jnp
        import numpy as np

        def _binarize(w):
            alpha = jax.lax.stop_gradient(jnp.mean(jnp.abs(w), axis=1, keepdims=True))
            bw = alpha * jnp.sign(w)
            return w + jax.lax.stop_gradient(bw - w)
        key = jax.random.key(seed)
        k1, k2, k3, k4, k5 = jax.random.split(key, 5)
        D, H = (256, 1024)
        x = jax.random.normal(k1, (64, 196, D), dtype=jnp.float32)
        w1 = jax.random.normal(k2, (H, D), dtype=jnp.float32) * 0.02
        b1 = jax.random.normal(k3, (H,), dtype=jnp.float32) * 0.02
        w2 = jax.random.normal(k4, (D, H), dtype=jnp.float32) * 0.02
        b2 = jax.random.normal(k5, (D,), dtype=jnp.float32) * 0.02
        return {'x': x, 'w1': w1, 'b1': b1, 'w2': w2, 'b2': b2}
    _L0_ffn_in = _L0_ffn_setup()
    _d = {'L0_attn_hidden_states': _L0_attn_in['hidden_states'], 'L0_attn_mu0': _L0_attn_in['mu0'], 'L0_attn_W_x0': _L0_attn_in['W_x0'], 'L0_attn_W_x2': _L0_attn_in['W_x2'], 'L0_attn_x_bias': _L0_attn_in['x_bias'], 'L0_attn_W_r': _L0_attn_in['W_r'], 'L0_attn_W_w1': _L0_attn_in['W_w1'], 'L0_attn_W_w2': _L0_attn_in['W_w2'], 'L0_attn_b_w2': _L0_attn_in['b_w2'], 'L0_attn_W_k': _L0_attn_in['W_k'], 'L0_attn_W_v': _L0_attn_in['W_v'], 'L0_attn_W_g': _L0_attn_in['W_g'], 'L0_attn_bonus': _L0_attn_in['bonus'], 'L0_attn_gn_weight': _L0_attn_in['gn_weight'], 'L0_attn_gn_bias': _L0_attn_in['gn_bias'], 'L0_attn_W_o': _L0_attn_in['W_o'], 'L0_ffn_w1': _L0_ffn_in['w1'], 'L0_ffn_b1': _L0_ffn_in['b1'], 'L0_ffn_w2': _L0_ffn_in['w2'], 'L0_ffn_b2': _L0_ffn_in['b2']}
    _x0 = _d['L0_attn_hidden_states']
    _d['L0_attn_hidden_states'] = jax.random.normal(jax.random.fold_in(jax.random.key(seed), 1), (16, 512, 256), dtype=_x0.dtype)
    del _x0
    return _d

def reference(L0_attn_hidden_states, L0_attn_mu0, L0_attn_W_x0, L0_attn_W_x2, L0_attn_x_bias, L0_attn_W_r, L0_attn_W_w1, L0_attn_W_w2, L0_attn_b_w2, L0_attn_W_k, L0_attn_W_v, L0_attn_W_g, L0_attn_bonus, L0_attn_gn_weight, L0_attn_gn_bias, L0_attn_W_o, L0_ffn_w1, L0_ffn_b1, L0_ffn_w2, L0_ffn_b2):

    def _L0_attn_ref(hidden_states, mu0, W_x0, W_x2, x_bias, W_r, W_w1, W_w2, b_w2, W_k, W_v, W_g, bonus, gn_weight, gn_bias, W_o):
        import jax, jax.numpy as jnp
        import numpy as np
        B, T, HID = (4, 512, 256)
        NH = 4
        KD, VD = (128, 256)
        DK, DV = (KD // NH, VD // NH)
        R = 32
        GLR = 64
        EPS = 1e-05

        def _rwkv6_scan(r, k, v, w, u):

            def step(S, xs):
                r_t, k_t, v_t, w_t = xs
                kv = k_t[..., :, None] * v_t[..., None, :]
                o_t = jnp.einsum('bhk,bhkv->bhv', r_t, S + u[None, :, :, None] * kv)
                S = jnp.exp(w_t)[..., None] * S + kv
                return (S, o_t)
            S0 = jnp.zeros(r.shape[:2] + (r.shape[-1], v.shape[-1]), r.dtype)
            mv = lambda x: jnp.moveaxis(x, 2, 0)
            _, o = jax.lax.scan(step, S0, (mv(r), mv(k), mv(v), mv(w)))
            return jnp.moveaxis(o, 0, 2)
        x = hidden_states
        shifted = jnp.pad(x, ((0, 0), (1, 0), (0, 0)))[:, :-1]
        delta = shifted - x
        xp = jnp.tanh((x + delta * mu0) @ W_x0.T)
        xp = xp.reshape(x.shape[0], x.shape[1], 5, R)
        mus = jnp.einsum('blnr,hnr->blnh', xp, W_x2.reshape(HID, 5, R)) + x_bias
        mu_r, mu_w, mu_k, mu_v, mu_g = (mus[:, :, i] for i in range(5))
        r = (x + delta * mu_r) @ W_r.T
        w = jnp.tanh((x + delta * mu_w) @ W_w1.T) @ W_w2.T + b_w2
        k = (x + delta * mu_k) @ W_k.T
        v = (x + delta * mu_v) @ W_v.T
        g = (x + delta * mu_g) @ W_g.T
        split = lambda t, d: t.reshape(t.shape[0], t.shape[1], NH, d).transpose(0, 2, 1, 3)
        r_, k_, w_ = (split(r, DK), split(k, DK), split(w, DK))
        v_ = split(v, DV)
        w_ = -jnp.exp(w_)
        o = _rwkv6_scan(r_, k_, v_, w_, bonus)
        o = o.transpose(0, 2, 1, 3)
        mean = o.mean(-1, keepdims=True)
        var = o.var(-1, keepdims=True)
        o = (o - mean) * jax.lax.rsqrt(var + EPS)
        o = o.reshape(x.shape[0], x.shape[1], VD) * gn_weight + gn_bias
        o = o * jax.nn.silu(g)
        return o @ W_o.T

    def _L0_ffn_ref(x, w1, b1, w2, b2):
        import jax, jax.numpy as jnp
        import numpy as np

        def _binarize(w):
            alpha = jax.lax.stop_gradient(jnp.mean(jnp.abs(w), axis=1, keepdims=True))
            bw = alpha * jnp.sign(w)
            return w + jax.lax.stop_gradient(bw - w)
        bw1 = _binarize(w1)
        h = jnp.einsum('bsd,hd->bsh', x, bw1) + b1
        h = jax.nn.gelu(h, approximate=False)
        bw2 = _binarize(w2)
        out = jnp.einsum('bsh,dh->bsd', h, bw2) + b2
        return out
    x = L0_attn_hidden_states
    xn = _layernorm(x, axis=-1)
    s = _L0_attn_ref(xn, L0_attn_mu0, L0_attn_W_x0, L0_attn_W_x2, L0_attn_x_bias, L0_attn_W_r, L0_attn_W_w1, L0_attn_W_w2, L0_attn_b_w2, L0_attn_W_k, L0_attn_W_v, L0_attn_W_g, L0_attn_bonus, L0_attn_gn_weight, L0_attn_gn_bias, L0_attn_W_o)
    g = _silu(_L0_ffn_ref(xn, L0_ffn_w1, L0_ffn_b1, L0_ffn_w2, L0_ffn_b2))
    x = x + s * g
    return x

_drawn_inputs = setup_inputs


def setup_inputs(seed=0):
    import zlib

    import numpy as np

    out = dict(_drawn_inputs(seed))
    spreads = {}
    factors = {'L0_attn_mu0': 8.0,
     'L0_attn_W_x0': 8.0,
     'L0_attn_W_x2': 8.0,
     'L0_attn_x_bias': 8.0,
     'L0_attn_W_r': 8.0,
     'L0_attn_W_w1': 8.0,
     'L0_attn_W_w2': 8.0,
     'L0_attn_b_w2': 8.0,
     'L0_attn_W_k': 8.0,
     'L0_attn_W_v': 8.0,
     'L0_attn_W_g': 8.0,
     'L0_attn_bonus': 8.0,
     'L0_attn_gn_weight': 8.0,
     'L0_attn_gn_bias': 8.0,
     'L0_attn_W_o': 8.0,
     'L0_ffn_w1': 8.0,
     'L0_ffn_b1': 8.0,
     'L0_ffn_w2': 8.0,
     'L0_ffn_b2': 8.0}
    for name, (base, spread) in spreads.items():
        noise = np.random.default_rng([zlib.crc32(name.encode()), seed]).standard_normal(out[name].shape)
        drawn = base * np.exp(spread * noise) if base else spread * noise
        out[name] = jnp.asarray(drawn.astype(out[name].dtype))
    for name, factor in factors.items():
        out[name] = (out[name] * factor).astype(out[name].dtype)
    return out
```

```python
from contextlib import ExitStack

import concourse.bass as bass
from concourse import mybir

ALU = mybir.AluOpType
ACT = mybir.ActivationFunctionType
AX_X = mybir.AxisListType.X
F32 = mybir.dt.float32
F16 = mybir.dt.float16
U8 = mybir.dt.uint8

P = 128
LN_EPS = 1e-5
GN_EPS = 1e-5


def rwkv6_gated_ffn(nc, x, mu0, wx0, wx2, x_bias, wr, ww1, ww2, b_w2, wk, wv, wg, bonus,
                    gn_w, gn_b, wo, w1_rows, w1_cols, b1, w2_rows, w2_cols, b2,
                    ident, level_masks, head_ones, out):
    B, T, HID = x.shape
    HB = HID // P
    C = T // P
    NH = head_ones.shape[1]
    DK = P // NH
    DV = wv.shape[2] // NH
    VD = NH * DV
    NMU = x_bias.shape[2]
    R = wx0.shape[2] // NMU
    GLR = ww2.shape[0] // 2
    MT = w1_rows.shape[1]
    L = P.bit_length() - 1
    HALF = P // 2
    CH = C * NH
    MW, MR, MK, MV, MG = 1, 0, 2, 3, 4
    ORDER = (MW, MR, MK, MV, MG)

    with ExitStack() as ctx:
        def sb(name, shape, dt):
            return ctx.enter_context(nc.sbuf_tensor(name, shape, dt))

        def sem(name):
            return ctx.enter_context(nc.semaphore(name))

        front_ps = ctx.enter_context(nc.psum_tensor("front_ps", [P, 2 * 512], F32))
        back_ps = ctx.enter_context(nc.psum_tensor("back_ps", [P, 2 * 512], F32))
        hid_ps = ctx.enter_context(nc.psum_tensor("hid_ps", [P, 2, T], F32))
        ffn_ps = ctx.enter_context(nc.psum_tensor("ffn_ps", [P, HB, T], F32))

        mu0_s = sb("mu0_s", [P, HB], F32)
        wx0_f = sb("wx0_f", [P, HB, NMU * R], F32)
        wx0_h = sb("wx0_h", [P, HB, NMU * R], F16)
        wx0_l = sb("wx0_l", [P, HB, NMU * R], F16)
        wx2_f = sb("wx2_f", [P, NMU, HID], F32)
        wx2_s = sb("wx2_s", [P, NMU, HID], F16)
        xb_s = sb("xb_s", [P, HB, NMU], F32)
        wr_s = sb("wr_s", [P, HB, P], F32)
        wk_s = sb("wk_s", [P, HB, P], F32)
        ww1_s = sb("ww1_s", [P, HB, P], F32)
        ww2_f = sb("ww2_f", [P, P], F32)
        ww2_h = sb("ww2_h", [P, P], F16)
        ww2_l = sb("ww2_l", [P, P], F16)
        bw2_s = sb("bw2_s", [P, 1], F32)
        wv_s = sb("wv_s", [P, HB, VD], F32)
        wv_mean = sb("wv_mean", [P, HB * NH], F32)
        wg_s = sb("wg_s", [P, HB, VD], F32)
        wo_s = sb("wo_s", [P, HB, HID], F32)
        u_s = sb("u_s", [P, 1], F32)
        gnw_s = sb("gnw_s", [P, HB], F32)
        gnb_s = sb("gnb_s", [P, HB], F32)
        b1_s = sb("b1_s", [P, MT], F32)
        b2_s = sb("b2_s", [P, HB], F32)
        alpha1 = sb("alpha1", [P, MT], F32)
        alpha2 = sb("alpha2", [P, HB], F32)
        sign1 = sb("sign1", [P, HB, MT * P], F16)
        sign2 = sb("sign2", [P, MT, HID], F16)
        ident_s = sb("ident_s", [P, P], F32)
        identm_s = sb("identm_s", [P, P], U8)
        masks_s = sb("masks_s", [P, L, HALF], U8)
        ones_s = sb("ones_s", [P, NH], F32)

        xt = sb("xt", [P, C, HID], F32)
        stats = sb("stats", [P, C, 6], F32)
        meanvar = sb("meanvar", [P, C, 2], F32)
        var_eps = sb("var_eps", [P, C], F32)
        rstd = sb("rstd", [P, C], F32)
        minus_half = sb("minus_half", [P, CH], F32)
        xnT = sb("xnT", [P, HB, T + 1], F32)
        xh = sb("xh", [P, HB, T], F16)
        xl = sb("xl", [P, HB, T], F16)
        delta = sb("delta", [P, HB, T], F32)
        y0 = sb("y0", [P, HB, T], F32)
        y0h = sb("y0h", [P, HB, T], F16)
        y0l = sb("y0l", [P, HB, T], F16)
        xpt = sb("xpt", [P, 2, T], F32)
        xph = sb("xph", [P, 2, T], F16)
        xpl = sb("xpl", [P, 2, T], F16)
        xps = sb("xps", [P, NMU, T], F16)
        yt = sb("yt", [P, 2, HB * T], F32)
        yy = sb("yy", [P, 2, HB * T], F32)
        wt = sb("wt", [P, T], F32)
        wst = sb("wst", [P, T], F16)
        ew = sb("ew", [P, T], F32)
        dF = sb("dF", [P, T], F32)
        rkF = sb("rkF", [P, 2, T], F32)
        vF = sb("vF", [P, C, VD], F32)
        sg = sb("sg", [P, HB, T], F32)
        hf = sb("hf", [P, 2, T], F32)
        hh = sb("hh", [P, 2, T], F16)
        hl = sb("hl", [P, 2, T], F16)
        zh = sb("zh", [P, HB, T], F32)
        gate = sb("gate", [P, HB, T], F32)

        xres = sb("xres", [P, C, HID], F32)
        Rw = sb("Rw", [P, T], F32)
        Kw = sb("Kw", [P, 2, T], F32)
        Dw = [dF] + [sb(f"D{l}", [P, T >> l], F32) for l in range(1, L + 1)]
        zd = sb("zd", [P, T], F32)
        Rx = sb("Rx", [P, 2, CH * HALF], F32)
        PT = sb("PT", [P, CH * P], F32)
        Ph = sb("Ph", [P, CH * P], F16)
        Pl = sb("Pl", [P, CH * P], F16)
        Rh = sb("Rh", [P, T], F16)
        Rl = sb("Rl", [P, T], F16)
        Kth = sb("Kth", [P, C - 1, P], F16)
        Ktl = sb("Ktl", [P, C - 1, P], F16)
        vh = sb("vh", [P, C, VD], F16)
        vl = sb("vl", [P, C, VD], F16)
        St = sb("St", [P, C - 1, DV], F32)
        Sxh = sb("Sxh", [P, C - 1, NH, DV], F16)
        Sxl = sb("Sxl", [P, C - 1, NH, DV], F16)
        on = sb("on", [P, CH, DV], F32)
        ss = sb("ss", [P, CH], F32)
        rs = sb("rs", [P, CH], F32)
        og = sb("og", [P, HB, T], F32)
        sgt = sb("sgt", [P, HB, T], F32)

        w1_rows_s = PT[:, :].rearrange("p (m k) -> p m k", m=MT)
        w1_cols_s = Rx[:, :, :].rearrange("p a b -> p (a b)")
        w2_rows_s = yt[:, :, :]
        masks_f = sgt[:, :, :].rearrange("p a b -> p (a b)")[:, 0:L * HALF]
        w2_cols_s = yy[:, :, :].rearrange("p a b -> p (a b)")

        loads = [(mu0_s, mu0), (wx0_f, wx0), (wx2_f, wx2), (xb_s, x_bias), (wr_s, wr), (wk_s, wk),
                 (ww1_s, ww1), (ww2_f, ww2), (bw2_s, b_w2), (wv_s, wv), (wg_s, wg), (wo_s, wo),
                 (u_s, bonus), (gnw_s, gn_w), (gnb_s, gn_b), (b1_s, b1), (b2_s, b2),
                 (ident_s, ident), (masks_f, level_masks), (ones_s, head_ones)]

        const_loaded = sem("const_loaded")
        ffn_w_loaded = sem("ffn_w_loaded")
        abs_done = sem("abs_done")
        sign_done = sem("sign_done")
        su = sem("su")
        setup_dve = sem("setup_dve")
        setup_pool = sem("setup_pool")

        x_loaded = sem("x_loaded")
        ln_stats = sem("ln_stats")
        ln_aggr = sem("ln_aggr")
        ln_var = sem("ln_var")
        ln_rstd = sem("ln_rstd")
        xn_ready = sem("xn_ready")
        xnT_psum = sem("xnT_psum")
        xnT_ready = sem("xnT_ready")
        xh_ready = sem("xh_ready")
        xl_ready = sem("xl_ready")
        delta_ready = sem("delta_ready")
        y0_ready = sem("y0_ready")
        y0h_ready = sem("y0h_ready")
        y0l_ready = sem("y0l_ready")
        xp_psum = sem("xp_psum")
        xp_tanh = sem("xp_tanh")
        xph_ready = sem("xph_ready")
        xpl_ready = sem("xpl_ready")
        xps_loaded = sem("xps_loaded")
        mus_psum = sem("mus_psum")
        yt_ready = sem("yt_ready")
        y_ready = sem("y_ready")
        w1_psum = sem("w1_psum")
        wt_ready = sem("wt_ready")
        wsth_ready = sem("wsth_ready")
        wst_ready = sem("wst_ready")
        w2_psum = sem("w2_psum")
        ew_ready = sem("ew_ready")
        d_ready = sem("d_ready")
        r_psum = sem("r_psum")
        r_ready = sem("r_ready")
        k_psum = sem("k_psum")
        k_ready = sem("k_ready")
        v_psum = sem("v_psum")
        v_ready = sem("v_ready")
        g_psum = sem("g_psum")
        tg_ready = sem("tg_ready")
        sg_ready = sem("sg_ready")
        hid_psum = sem("hid_psum")
        gelu_done = sem("gelu_done")
        hh_ready = sem("hh_ready")
        hl_ready = sem("hl_ready")
        ffn2_done = sem("ffn2_done")
        zh_ready = sem("zh_ready")
        tz_ready = sem("tz_ready")
        gate_ready = sem("gate_ready")
        xres_loaded = sem("xres_loaded")
        rk_taken = sem("rk_taken")
        zd_ready = sem("zd_ready")
        D_ready = sem("D_ready")
        diag_psum = sem("diag_psum")
        diag_done = sem("diag_done")
        rx_ready = sem("rx_ready")
        lev_psum = sem("lev_psum")
        sel_done = sem("sel_done")
        r_upd = sem("r_upd")
        k_upd = sem("k_upd")
        vh_ready = sem("vh_ready")
        vl_ready = sem("vl_ready")
        Rh_ready = sem("Rh_ready")
        Rl_ready = sem("Rl_ready")
        kt_psum = sem("kt_psum")
        kth_ready = sem("kth_ready")
        ktl_ready = sem("ktl_ready")
        u_psum = sem("u_psum")
        st_ready = sem("st_ready")
        sxh_ready = sem("sxh_ready")
        sxl_ready = sem("sxl_ready")
        ph_ready = sem("ph_ready")
        pl_ready = sem("pl_ready")
        o_psum = sem("o_psum")
        osq_ready = sem("osq_ready")
        ss_ready = sem("ss_ready")
        ss_eps_ready = sem("ss_eps_ready")
        rs_ready = sem("rs_ready")
        on_ready = sem("on_ready")
        oT_psum = sem("oT_psum")
        oT_ready = sem("oT_ready")
        og_ready = sem("og_ready")
        s_psum = sem("s_psum")
        sgt_ready = sem("sgt_ready")
        outT_psum = sem("outT_psum")
        out_ready = sem("out_ready")
        stored = sem("stored")

        x_tok = x.rearrange("b (c p) h -> b p c h", p=P)
        out_tok = out.rearrange("b (c p) h -> b p c h", p=P)

        def wait(eng, s, value):
            if not (isinstance(value, int) and value <= 0):
                eng.wait_ge(s, value)

        def blocks(ap, half, m):
            return ap.rearrange("p (b two m) -> p b two m", two=2, m=m)[:, :, half, :]

        def rows(eng, body):
            body((1, 0, 0), None)
            body((2, 1, 1), (1, 0, 0))
            with eng.Fori(2, B) as i:
                before = eng.snap(i - 1)
                here = eng.snap(i + 0)
                after = eng.snap(i + 1)
                body((after, here, here), (here, before, before))
            body(None, (B, B - 1, B - 1))

        block = ctx.enter_context(nc.Block())

        @block.sync
        def _(sp):
            for dst, src in loads:
                sp.dma_start(dst if dst is masks_f else dst[:], src).then_inc(const_loaded, 16)

            def body(F, K):
                if F:
                    n, p, i = F
                    wait(sp, xnT_psum, p)
                    sp.dma_start(xt[:, :, :], x_tok[i]).then_inc(x_loaded, 16)
                if K:
                    n, p, j = K
                    wait(sp, stored, 16 * p)
                    sp.dma_start(xres[:, :, :], x_tok[j]).then_inc(xres_loaded, 16)
                if F:
                    n, p, i = F
                    for part, ready, quadrants in ((xph, xph_ready, (0, 1)), (xpl, xpl_ready, (2, 3))):
                        sp.wait_ge(ready, n)
                        if part is xph:
                            wait(sp, sg_ready, p)
                        for q in quadrants:
                            for k in range(NMU):
                                a, row = (0, R * k) if k < 4 else (1, 0)
                                sp.dma_start(xps[R * q:R * q + R, k, :], part[row:row + R, a, :])\
                                    .then_inc(xps_loaded, 16)
                if K:
                    n, p, j = K
                    wait(sp, out_ready, n)
                    sp.dma_start(out_tok[j], xres[:, :, :]).then_inc(stored, 16)

            rows(sp, body)
            sp.wait_ge(stored, 16 * B)

        @block.scalar
        def _(act):
            act.dma_start(w1_rows_s, w1_rows).then_inc(ffn_w_loaded, 16)
            act.dma_start(w2_rows_s, w2_rows).then_inc(ffn_w_loaded, 16)
            act.dma_start(w1_cols_s, w1_cols).then_inc(ffn_w_loaded, 16)
            act.dma_start(w2_cols_s, w2_cols).then_inc(ffn_w_loaded, 16)
            act.wait_ge(ffn_w_loaded, 64)
            act.activation(w1_rows_s, w1_rows_s, ACT.Abs).then_inc(abs_done, 1)
            act.activation(w2_rows_s, w2_rows_s, ACT.Abs).then_inc(abs_done, 1)
            act.activation(sign1[:, :, :].rearrange("p a b -> p (a b)"), w1_cols_s, ACT.Sign)
            act.activation(sign2[:, :, :].rearrange("p a b -> p (a b)"), w2_cols_s, ACT.Sign)\
                .then_inc(sign_done, 1)
            act.wait_ge(setup_dve, 1)
            act.wait_ge(setup_pool, 1)

            def gelu(F, m):
                n, p, _ = F
                act.wait_ge(hid_psum, MT * p + m + 1)
                wait(act, hl_ready, MT * p + max(m - 1, 0))
                act.activation(hf[:, m % 2, :], hid_ps[:, m % 2, :], ACT.Gelu, bias=b1_s[:, m:m + 1],
                               scale=alpha1[:, m:m + 1]).then_inc(gelu_done, 1)

            def expand(K, l):
                n, p, _ = K
                m = 1 << l
                if l:
                    act.wait_ge(r_upd, L * p + l)
                else:
                    act.wait_ge(rk_taken, n)
                wait(act, lev_psum, L * p + max(l - 1, 0))
                for h in range(NH):
                    q = slice(DK * h, DK * h + DK)
                    src = Rw[q, :].rearrange("p (c b two m) -> p c b two m", c=C, two=2, m=m)[:, :, :, 1, :]
                    dst = Rx[q, l % 2, :].rearrange("p (c h b m) -> p c h b m", c=C, h=NH, m=m)[:, :, h, :, :]
                    last = act.activation(dst, src, ACT.Copy)
                last.then_inc(rx_ready, 1)

            def body(F, K):
                if F:
                    n, p, _ = F
                    act.wait_ge(xnT_psum, n)
                    wait(act, y_ready, NMU * p)
                    act.activation(xnT[:, :, 1:T + 1],
                                   front_ps[:, :].rearrange("p (a t) -> p a t", a=HB), ACT.Copy)\
                        .then_inc(xnT_ready, 1)
                    wait(act, hid_psum, MT * p)
                    act.activation(xh[:, :, :], front_ps[:, :].rearrange("p (a t) -> p a t", a=HB),
                                   ACT.Copy).then_inc(xh_ready, 1)
                if K:
                    expand(K, 0)
                if F:
                    gelu(F, 0)
                if K:
                    expand(K, 1)
                if F:
                    gelu(F, 1)
                    n, p, _ = F
                    act.wait_ge(xp_psum, n)
                    wait(act, xpl_ready, p)
                    act.activation(xpt[:, 0, :], front_ps[:, 0:T], ACT.Tanh)
                    act.activation(xpt[0:R, 1, :], front_ps[0:R, T:2 * T], ACT.Tanh).then_inc(xp_tanh, 1)
                if K:
                    expand(K, 2)
                if F:
                    gelu(F, 2)
                if K:
                    expand(K, 3)
                if F:
                    gelu(F, 3)
                if K:
                    expand(K, 4)
                if F:
                    gelu(F, 4)
                    n, p, _ = F
                    act.wait_ge(w1_psum, n)
                    wait(act, wst_ready, p)
                    act.activation(wt[:, :], front_ps[:, 0:T], ACT.Tanh).then_inc(wt_ready, 1)
                if K:
                    expand(K, 5)
                if F:
                    gelu(F, 5)
                if K:
                    expand(K, 6)
                if F:
                    n, p, _ = F
                    act.wait_ge(w2_psum, n)
                    act.activation(ew[:, :], front_ps[:, 0:T], ACT.Exp, bias=bw2_s[:, 0:1])\
                        .then_inc(ew_ready, 1)
                    act.wait_ge(ew_ready, n)
                    wait(act, k_upd, L * (p - 1) + 1)
                    wait(act, r_upd, L * (p - 1) + 1)
                    act.activation(dF[:, :], ew[:, :], ACT.Exp, scale=-1.0).then_inc(d_ready, 1)
                    act.wait_ge(r_psum, n)
                    wait(act, rk_taken, p)
                    act.activation(rkF[:, 0, :], front_ps[:, T:2 * T], ACT.Copy).then_inc(r_ready, 1)
                if K:
                    n, p, _ = K
                    act.wait_ge(sel_done, L * n)
                    wait(act, o_psum, p)
                    act.activation(Ph[:, :], PT[:, :], ACT.Copy).then_inc(ph_ready, 1)
                if F:
                    gelu(F, 6)
                    n, p, _ = F
                    act.wait_ge(k_psum, n)
                    act.activation(rkF[:, 1, :], front_ps[:, 0:T], ACT.Copy).then_inc(k_ready, 1)
                    gelu(F, 7)
                if K:
                    n, p, _ = K
                    act.wait_ge(o_psum, n)
                    wait(act, oT_psum, p)
                    act.activation(on[:, :, :].rearrange("p a b -> p (a b)"), back_ps[:, :], ACT.Square)\
                        .then_inc(osq_ready, 1)
                if F:
                    n, p, _ = F
                    act.wait_ge(v_psum, n)
                    wait(act, vl_ready, p)
                    act.activation(vF[:, :, :].rearrange("p a b -> p (a b)"), front_ps[:, :], ACT.Copy)\
                        .then_inc(v_ready, 1)
                if K:
                    n, p, _ = K
                    act.wait_ge(oT_psum, n)
                    wait(act, s_psum, p)
                    for a in range(HB):
                        last = act.activation(og[:, a, :], back_ps[:, a * T:(a + 1) * T], ACT.Identity,
                                              bias=gnb_s[:, a:a + 1], scale=gnw_s[:, a:a + 1])
                    last.then_inc(oT_ready, 1)
                if F:
                    n, p, _ = F
                    act.wait_ge(g_psum, n)
                    wait(act, og_ready, p)
                    act.activation(sg[:, :, :], front_ps[:, :].rearrange("p (a t) -> p a t", a=HB),
                                   ACT.Tanh, scale=0.5).then_inc(tg_ready, 1)
                    act.wait_ge(ffn2_done, MT * n)
                    wait(act, gate_ready, p)
                    for a in range(HB):
                        last = act.activation(zh[:, a, :], ffn_ps[:, a, :], ACT.Identity,
                                              bias=b2_s[:, a:a + 1], scale=alpha2[:, a:a + 1])
                    last.then_inc(zh_ready, 1)
                    act.wait_ge(zh_ready, n)
                    wait(act, sgt_ready, p)
                    act.activation(gate[:, :, :], zh[:, :, :], ACT.Tanh).then_inc(tz_ready, 1)

            rows(act, body)

        @block.gpsimd
        def _(pool):
            pool.memset(Sxh[:, :, :, :], 0.0)
            pool.memset(Sxl[:, :, :, :], 0.0)
            pool.memset(xnT[:, :, 0:1], 0.0)
            pool.memset(minus_half[:, :], -0.5)
            pool.wait_ge(abs_done, 2)
            pool.wait_ge(sign_done, 1)
            pool.memset(Rx[:, :, :], 0.0)
            pool.wait_ge(setup_dve, 1)
            pool.memset(PT[:, :], 0.0).then_inc(setup_pool, 1)

            def k_step(K, l):
                n, p, _ = K
                m = 1 << l
                if l:
                    pool.wait_ge(k_upd, L * p + l)
                else:
                    pool.wait_ge(rk_taken, n)
                if l:
                    pool.wait_ge(D_ready, L * p + l)
                else:
                    pool.wait_ge(d_ready, n)
                if l >= 1:
                    pool.wait_ge(lev_psum, L * p + l)
                else:
                    wait(pool, kt_psum, p)
                src, dst = Kw[:, l % 2, :], Kw[:, (l + 1) % 2, :]
                D2 = Dw[l][:, :].rearrange("p (b two) -> p b two", two=2)[:, :, 1:2]\
                    .to_broadcast([P, T // (2 * m), m])
                pool.tensor_tensor(blocks(dst, 0, m), blocks(src, 0, m), D2, ALU.mult)
                pool.tensor_copy(blocks(dst, 1, m), blocks(src, 1, m)).then_inc(k_upd, 1)

            def h_low(F, m):
                n, p, _ = F
                pool.wait_ge(hh_ready, MT * p + m + 1)
                wait(pool, ffn2_done, MT * p + max(m - 1, 0))
                pool.tensor_tensor(hl[:, m % 2, :], hf[:, m % 2, :], hh[:, m % 2, :], ALU.subtract)\
                    .then_inc(hl_ready, 1)

            def mix_sum(F, o):
                n, p, _ = F
                k = ORDER[o]
                pool.wait_ge(yt_ready, NMU * p + o + 1)
                used = (w1_psum, r_psum, k_psum, v_psum, g_psum)
                wait(pool, used[o - 2], n) if o >= 2 else wait(pool, used[4 - o], p)
                pool.tensor_tensor(yy[:, o % 2, :].rearrange("p (a t) -> p a t", a=HB),
                                   yt[:, o % 2, :].rearrange("p (a t) -> p a t", a=HB),
                                   xnT[:, :, 1:T + 1], ALU.add).then_inc(y_ready, 1)

            def body(F, K):
                if K:
                    k_step(K, 0)
                if F:
                    n, p, _ = F
                    pool.wait_ge(ln_var, n)
                    wait(pool, xn_ready, p)
                    pool.tensor_tensor(rstd[:, :], var_eps[:, :], minus_half[:, 0:C], ALU.pow)\
                        .then_inc(ln_rstd, 1)
                    pool.wait_ge(xnT_ready, n)
                    pool.wait_ge(xh_ready, n)
                    pool.tensor_tensor(xl[:, :, :], xnT[:, :, 1:T + 1], xh[:, :, :], ALU.subtract)\
                        .then_inc(xl_ready, 1)
                if K:
                    k_step(K, 1)
                if F:
                    h_low(F, 0)
                if K:
                    k_step(K, 2)
                if F:
                    h_low(F, 1)
                if K:
                    k_step(K, 3)
                if F:
                    h_low(F, 2)
                    mix_sum(F, 0)
                    h_low(F, 3)
                if K:
                    k_step(K, 4)
                if F:
                    mix_sum(F, 1)
                    h_low(F, 4)
                if K:
                    k_step(K, 5)
                if F:
                    mix_sum(F, 2)
                    h_low(F, 5)
                if K:
                    k_step(K, 6)
                if F:
                    mix_sum(F, 3)
                    h_low(F, 6)
                    mix_sum(F, 4)
                    h_low(F, 7)
                if K:
                    n, p, _ = K
                    pool.wait_ge(ss_eps_ready, n)
                    wait(pool, on_ready, p)
                    pool.tensor_tensor(rs[:, :], ss[:, :], minus_half[:, :], ALU.pow)\
                        .then_inc(rs_ready, 1)

            rows(pool, body)

        @block.vector
        def _(dve):
            step = [0]

            def then(ins):
                step[0] += 1
                ins.then_inc(su, 1)
                dve.wait_ge(su, step[0])

            dve.wait_ge(const_loaded, 16 * len(loads))
            dve.tensor_copy(identm_s[:, :], ident_s[:, :])
            dve.tensor_copy(masks_s[:, :, :].rearrange("p l t -> p (l t)"), masks_f)
            then(dve.tensor_copy(wx0_h[:, :, :], wx0_f[:, :, :]))
            dve.tensor_tensor(wx0_l[:, :, :], wx0_f[:, :, :], wx0_h[:, :, :], ALU.subtract)
            then(dve.tensor_copy(wx2_s[:, :, :], wx2_f[:, :, :]))
            for q in (1, 3):
                s = slice(R * q, R * q + R)
                dve.tensor_tensor(wx2_s[s, :, :], wx2_f[s, :, :], wx2_s[s, :, :], ALU.subtract)
            then(dve.tensor_copy(ww2_h[:, :], ww2_f[:, :]))
            dve.tensor_tensor(ww2_l[:, :], ww2_f[:, :], ww2_h[:, :], ALU.subtract)
            wv_heads = wv_s[:, :, :].rearrange("p a (h v) -> p (a h) v", v=DV)
            then(dve.tensor_reduce(wv_mean[:, :], wv_heads, AX_X, ALU.add))
            then(dve.tensor_scalar(wv_mean[:, :], wv_mean[:, :], 1.0 / DV, None, ALU.mult))
            dve.tensor_tensor(wv_heads, wv_heads,
                              wv_mean[:, :].unsqueeze(2).to_broadcast([P, HB * NH, DV]), ALU.subtract)
            dve.tensor_scalar(gnw_s[:, :], gnw_s[:, :], 0.5 * DV ** 0.5, None, ALU.mult)
            dve.tensor_scalar(gnb_s[:, :], gnb_s[:, :], 0.5, None, ALU.mult)
            dve.tensor_scalar(b2_s[:, :], b2_s[:, :], 0.5, None, ALU.mult)
            dve.wait_ge(abs_done, 2)
            then(dve.tensor_reduce(alpha1[:, :], w1_rows_s, AX_X, ALU.add))
            dve.tensor_scalar(alpha1[:, :], alpha1[:, :], 1.0 / HID, None, ALU.mult)
            then(dve.tensor_reduce(alpha2[:, :], w2_rows_s, AX_X, ALU.add))
            dve.tensor_scalar(alpha2[:, :], alpha2[:, :], 0.5 / (MT * P), None, ALU.mult)\
                .then_inc(setup_dve, 1)
            dve.wait_ge(setup_dve, 1)
            dve.wait_ge(setup_pool, 1)

            def h_high(F, m):
                n, p, _ = F
                dve.wait_ge(gelu_done, MT * p + m + 1)
                wait(dve, ffn2_done, MT * p + max(m - 1, 0))
                dve.tensor_copy(hh[:, m % 2, :], hf[:, m % 2, :]).then_inc(hh_ready, 1)

            def mix(F, o):
                n, p, _ = F
                k = ORDER[o]
                dve.wait_ge(mus_psum, NMU * p + o + 1)
                wait(dve, y_ready, NMU * p + max(o - 1, 0))
                for a in range(HB):
                    last = dve.scalar_tensor_tensor(yt[:, o % 2, a * T:(a + 1) * T],
                                                    front_ps[:, a * T:(a + 1) * T], xb_s[:, a, k:k + 1],
                                                    delta[:, a, :], ALU.add, ALU.mult)
                last.then_inc(yt_ready, 1)

            def select(K, l):
                n, p, _ = K
                m = 1 << l
                nb = HALF // m
                dve.wait_ge(setup_dve, 1)
                dve.wait_ge(lev_psum, L * p + l + 1)
                dst = PT[:, :].rearrange("p (g b two m) -> p g b two m", g=CH, two=2, m=m)[:, :, :, 1, :]
                src = back_ps[:, :].rearrange("p (g b m) -> p g b m", g=CH, m=m)
                msk = masks_s[:, l, :].rearrange("p (b m) -> p b m", m=m).unsqueeze(1)\
                    .to_broadcast([P, CH, nb, m])
                dve.copy_predicated(dst, msk, src).then_inc(sel_done, 1)

            def r_step(K, l):
                n, p, _ = K
                m = 1 << l
                dve.wait_ge(rx_ready, L * p + l + 1)
                if l:
                    dve.wait_ge(D_ready, L * p + l)
                    dve.wait_ge(r_upd, L * p + l)
                D1 = Dw[l][:, :].rearrange("p (b two) -> p b two", two=2)[:, :, 0:1]\
                    .to_broadcast([P, T // (2 * m), m])
                dve.tensor_tensor(blocks(Rw[:, :], 1, m), blocks(Rw[:, :], 1, m), D1, ALU.mult)\
                    .then_inc(r_upd, 1)

            def body(F, K):
                if K:
                    n, p, _ = K
                    dve.wait_ge(r_ready, n)
                    dve.wait_ge(k_ready, n)
                    wait(dve, Rl_ready, p)
                    dve.tensor_copy(Rw[:, :], rkF[:, 0, :])
                    wait(dve, lev_psum, L * p)
                    dve.tensor_copy(Kw[:, 0, :], rkF[:, 1, :]).then_inc(rk_taken, 1)
                    wait(dve, diag_psum, p)
                    dve.scalar_tensor_tensor(zd[:, :], rkF[:, 0, :], u_s[:, 0:1], rkF[:, 1, :],
                                             ALU.mult, ALU.mult).then_inc(zd_ready, 1)
                    dve.wait_ge(d_ready, n)
                    wait(dve, k_upd, L * p)
                    for l in range(1, L + 1):
                        pair = Dw[l - 1][:, :].rearrange("p (b two) -> p b two", two=2)
                        if l > 1:
                            dve.wait_ge(D_ready, L * p + l - 1)
                        dve.tensor_tensor(Dw[l][:, :], pair[:, :, 0], pair[:, :, 1], ALU.mult)\
                            .then_inc(D_ready, 1)
                if F:
                    n, p, _ = F
                    dve.wait_ge(x_loaded, 16 * n)
                    for c in range(C):
                        last = dve.bn_stats(stats[:, c, :], xt[:, c, :])
                    last.then_inc(ln_stats, 1)
                    dve.wait_ge(setup_dve, 1)
                    dve.wait_ge(ln_stats, n)
                    for c in range(C):
                        last = dve.bn_aggr(meanvar[:, c, :], stats[:, c, :])
                    last.then_inc(ln_aggr, 1)
                    dve.wait_ge(ln_aggr, n)
                    wait(dve, ln_rstd, p)
                    dve.tensor_scalar(var_eps[:, :], meanvar[:, :, 1], LN_EPS, None, ALU.add)\
                        .then_inc(ln_var, 1)
                    dve.wait_ge(ln_rstd, n)
                    for c in range(C):
                        last = dve.tensor_scalar(xt[:, c, :], xt[:, c, :], meanvar[:, c, 0:1],
                                                 rstd[:, c:c + 1], ALU.subtract, ALU.mult)
                    last.then_inc(xn_ready, 1)
                if K:
                    n, p, _ = K
                    dve.wait_ge(setup_dve, 1)
                    dve.wait_ge(diag_psum, n)
                    wait(dve, ph_ready, p)
                    wait(dve, pl_ready, p)
                    dve.copy_predicated(PT[:, :].rearrange("p (g t) -> p g t", g=CH),
                                        identm_s[:, :].unsqueeze(1).to_broadcast([P, CH, P]),
                                        back_ps[:, 0:CH].unsqueeze(2).to_broadcast([P, CH, P]))\
                        .then_inc(diag_done, 1)
                    r_step(K, 0)
                if F:
                    n, p, _ = F
                    dve.wait_ge(xnT_ready, n)
                    dve.tensor_tensor(delta[:, :, :], xnT[:, :, 0:T], xnT[:, :, 1:T + 1], ALU.subtract)\
                        .then_inc(delta_ready, 1)
                    dve.wait_ge(delta_ready, n)
                    for a in range(HB):
                        last = dve.scalar_tensor_tensor(y0[:, a, :], delta[:, a, :], mu0_s[:, a:a + 1],
                                                        xnT[:, a, 1:T + 1], ALU.mult, ALU.add)
                    last.then_inc(y0_ready, 1)
                    dve.wait_ge(y0_ready, n)
                    wait(dve, xp_psum, p)
                    dve.tensor_copy(y0h[:, :, :], y0[:, :, :]).then_inc(y0h_ready, 1)
                    dve.wait_ge(y0h_ready, n)
                    dve.tensor_tensor(y0l[:, :, :], y0[:, :, :], y0h[:, :, :], ALU.subtract)\
                        .then_inc(y0l_ready, 1)
                if K:
                    select(K, 0)
                    r_step(K, 1)
                if F:
                    h_high(F, 0)
                if K:
                    n, p, _ = K
                    dve.wait_ge(v_ready, n)
                    wait(dve, o_psum, p)
                    dve.tensor_copy(vh[:, :, :], vF[:, :, :]).then_inc(vh_ready, 1)
                    dve.wait_ge(vh_ready, n)
                    dve.tensor_tensor(vl[:, :, :], vF[:, :, :], vh[:, :, :], ALU.subtract)\
                        .then_inc(vl_ready, 1)
                    select(K, 1)
                    r_step(K, 2)
                if F:
                    h_high(F, 1)
                    n, p, _ = F
                    dve.wait_ge(xp_tanh, n)
                    wait(dve, xps_loaded, 16 * 4 * NMU * p)
                    dve.tensor_copy(xph[:, 0, :], xpt[:, 0, :])
                    dve.tensor_copy(xph[0:R, 1, :], xpt[0:R, 1, :]).then_inc(xph_ready, 1)
                    dve.wait_ge(xph_ready, n)
                    dve.tensor_tensor(xpl[:, 0, :], xpt[:, 0, :], xph[:, 0, :], ALU.subtract)
                    dve.tensor_tensor(xpl[0:R, 1, :], xpt[0:R, 1, :], xph[0:R, 1, :], ALU.subtract)\
                        .then_inc(xpl_ready, 1)
                if K:
                    select(K, 2)
                    r_step(K, 3)
                if F:
                    h_high(F, 2)
                    mix(F, 0)
                if K:
                    select(K, 3)
                    r_step(K, 4)
                if F:
                    h_high(F, 3)
                    mix(F, 1)
                if K:
                    select(K, 4)
                    r_step(K, 5)
                if F:
                    h_high(F, 4)
                    n, p, _ = F
                    dve.wait_ge(wt_ready, n)
                    wait(dve, w2_psum, p)
                    dve.tensor_copy(wst[:, :], wt[:, :]).then_inc(wsth_ready, 1)
                    dve.wait_ge(wsth_ready, n)
                    dve.tensor_tensor(wst[GLR:P, :], wt[GLR:P, :], wst[GLR:P, :], ALU.subtract)\
                        .then_inc(wst_ready, 1)
                    mix(F, 2)
                if K:
                    select(K, 5)
                    r_step(K, 6)
                if F:
                    h_high(F, 5)
                if K:
                    n, p, _ = K
                    dve.wait_ge(r_upd, L * n)
                    wait(dve, o_psum, p)
                    dve.tensor_copy(Rh[:, :], Rw[:, :]).then_inc(Rh_ready, 1)
                    dve.wait_ge(Rh_ready, n)
                    dve.tensor_tensor(Rl[:, :], Rw[:, :], Rh[:, :], ALU.subtract).then_inc(Rl_ready, 1)
                    select(K, 6)
                if F:
                    mix(F, 3)
                    h_high(F, 6)
                if K:
                    n, p, _ = K
                    dve.wait_ge(kt_psum, n)
                    wait(dve, u_psum, p)
                    kt_ps = back_ps[:, 0:(C - 1) * P].rearrange("p (c k) -> p c k", c=C - 1)
                    dve.tensor_copy(Kth[:, :, :], kt_ps).then_inc(kth_ready, 1)
                    dve.wait_ge(kth_ready, n)
                    dve.tensor_tensor(Ktl[:, :, :], kt_ps, Kth[:, :, :], ALU.subtract)\
                        .then_inc(ktl_ready, 1)
                    dve.wait_ge(ph_ready, n)
                    dve.tensor_tensor(Pl[:, :], PT[:, :], Ph[:, :], ALU.subtract).then_inc(pl_ready, 1)
                    dve.wait_ge(u_psum, n)
                    wait(dve, sxl_ready, p)
                    dve.tensor_copy(St[:, 0, :], back_ps[:, 0:DV]).then_inc(st_ready, 1)
                    for c in range(1, C - 1):
                        dve.wait_ge(st_ready, (C - 1) * p + c)
                        dve.scalar_tensor_tensor(St[:, c, :], St[:, c - 1, :], Dw[L][:, c:c + 1],
                                                 back_ps[:, c * DV:(c + 1) * DV], ALU.mult, ALU.add)\
                            .then_inc(st_ready, 1)
                    dve.wait_ge(st_ready, (C - 1) * n)
                    for h in range(NH):
                        q = slice(DK * h, DK * h + DK)
                        last = dve.tensor_copy(Sxh[q, :, h, :], St[q, :, :])
                    last.then_inc(sxh_ready, 1)
                    dve.wait_ge(sxh_ready, n)
                    for h in range(NH):
                        q = slice(DK * h, DK * h + DK)
                        last = dve.tensor_tensor(Sxl[q, :, h, :], St[q, :, :], Sxh[q, :, h, :],
                                                 ALU.subtract)
                    last.then_inc(sxl_ready, 1)
                if F:
                    mix(F, 4)
                    h_high(F, 7)
                if K:
                    n, p, _ = K
                    dve.wait_ge(osq_ready, n)
                    dve.tensor_reduce(ss[:, :], on[:, :, :], AX_X, ALU.add).then_inc(ss_ready, 1)
                    dve.wait_ge(ss_ready, n)
                    dve.tensor_scalar(ss[:, :], ss[:, :], DV * GN_EPS, None, ALU.add)\
                        .then_inc(ss_eps_ready, 1)
                    dve.wait_ge(rs_ready, n)
                    dve.tensor_tensor(on[:, :, :], back_ps[:, :].rearrange("p (g v) -> p g v", v=DV),
                                      rs[:, :].unsqueeze(2).to_broadcast([P, CH, DV]), ALU.mult)\
                        .then_inc(on_ready, 1)
                    dve.wait_ge(oT_ready, n)
                    dve.wait_ge(sg_ready, n)
                    dve.tensor_tensor(og[:, :, :], og[:, :, :], sg[:, :, :], ALU.mult)\
                        .then_inc(og_ready, 1)
                if F:
                    n, p, _ = F
                    dve.wait_ge(tg_ready, n)
                    dve.scalar_tensor_tensor(sg[:, :, :], sg[:, :, :], 1.0,
                                             front_ps[:, :].rearrange("p (a t) -> p a t", a=HB),
                                             ALU.add, ALU.mult).then_inc(sg_ready, 1)
                if K:
                    n, p, _ = K
                    dve.wait_ge(s_psum, n)
                    dve.wait_ge(gate_ready, n)
                    wait(dve, outT_psum, p)
                    dve.tensor_tensor(sgt[:, :, :], back_ps[:, :].rearrange("p (a t) -> p a t", a=HB),
                                      gate[:, :, :], ALU.mult).then_inc(sgt_ready, 1)
                if F:
                    n, p, _ = F
                    dve.wait_ge(tz_ready, n)
                    dve.scalar_tensor_tensor(gate[:, :, :], gate[:, :, :], 1.0, zh[:, :, :],
                                             ALU.add, ALU.mult).then_inc(gate_ready, 1)
                if K:
                    n, p, _ = K
                    dve.wait_ge(outT_psum, n)
                    dve.wait_ge(xres_loaded, 16 * n)
                    dve.tensor_tensor(xres[:, :, :], back_ps[:, :].rearrange("p (c h) -> p c h", c=C),
                                      xres[:, :, :], ALU.add).then_inc(out_ready, 1)

            rows(dve, body)

        @block.tensor
        def _(pe):
            pe.wait_ge(setup_dve, 1)
            pe.wait_ge(setup_pool, 1)
            pe.wait_ge(sign_done, 1)

            def mm(dst, pairs, start=True, stop=True):
                for k, (a, b) in enumerate(pairs):
                    last = pe.matmul(dst, a, b, start=start and k == 0, stop=stop and k == len(pairs) - 1,
                                     skip_group_check=True)
                return last

            def ffn1(F, m):
                n, p, _ = F
                if m == 0:
                    pe.wait_ge(xh_ready, n)
                    pe.wait_ge(xl_ready, n)
                wait(pe, gelu_done, MT * p + max(m - 1, 0))
                mm(hid_ps[:, m % 2, :], [(sign1[:, a, m * P:(m + 1) * P], part[:, a, :])
                                         for a in range(HB) for part in (xh, xl)]).then_inc(hid_psum, 1)

            def ffn2(F, m):
                n, p, _ = F
                if m == 0:
                    wait(pe, zh_ready, p)
                pe.wait_ge(hh_ready, MT * p + m + 1)
                pe.wait_ge(hl_ready, MT * p + m + 1)
                for a in range(HB):
                    last = mm(ffn_ps[:, a, :], [(sign2[:, m, a * P:(a + 1) * P], part[:, m % 2, :])
                                                for part in (hh, hl)], start=m == 0, stop=m == MT - 1)
                last.then_inc(ffn2_done, 1)

            def level(K, l):
                n, p, _ = K
                pe.wait_ge(rx_ready, L * p + l + 1)
                if l:
                    pe.wait_ge(k_upd, L * p + l)
                    pe.wait_ge(sel_done, L * p + l)
                else:
                    pe.wait_ge(rk_taken, n)
                    pe.wait_ge(diag_done, n)
                for c in range(C):
                    last = mm(back_ps[:, c * NH * HALF:(c + 1) * NH * HALF],
                              [(Kw[:, l % 2, c * P:(c + 1) * P],
                                Rx[:, l % 2, c * NH * HALF:(c + 1) * NH * HALF])])
                last.then_inc(lev_psum, 1)

            def mus(F, o):
                n, p, _ = F
                k = ORDER[o]
                for a in range(HB):
                    last = mm(front_ps[:, a * T:(a + 1) * T], [(wx2_s[:, k, a * P:(a + 1) * P], xps[:, k, :])])
                last.then_inc(mus_psum, 1)

            def project(dst, w, o):
                return mm(dst, [(w[:, a, :], yy[:, o % 2, a * T:(a + 1) * T]) for a in range(HB)])

            def body(F, K):
                if K:
                    n, p, _ = K
                    pe.wait_ge(zd_ready, n)
                    wait(pe, out_ready, p)
                    for c in range(C):
                        last = mm(back_ps[:, c * NH:(c + 1) * NH], [(zd[:, c * P:(c + 1) * P], ones_s[:, :])])
                    last.then_inc(diag_psum, 1)
                if F:
                    n, p, _ = F
                    pe.wait_ge(xn_ready, n)
                    wait(pe, sg_ready, p)
                    for c in range(C):
                        for a in range(HB):
                            last = pe.transpose(front_ps[:, a * T + c * P:a * T + (c + 1) * P],
                                                xt[:, c, a * P:(a + 1) * P], ident_s[:, :])
                    last.then_inc(xnT_psum, 1)
                if K:
                    level(K, 0)
                if F:
                    ffn1(F, 0)
                if K:
                    level(K, 1)
                if F:
                    ffn1(F, 1)
                    n, p, _ = F
                    pe.wait_ge(y0l_ready, n)
                    for dst, cols in ((front_ps[:, 0:T], slice(0, P)),
                                      (front_ps[0:R, T:2 * T], slice(P, NMU * R))):
                        last = mm(dst, [(w[:, a, cols], y[:, a, :]) for a in range(HB)
                                        for w, y in ((wx0_h, y0h), (wx0_l, y0h), (wx0_h, y0l))])
                    last.then_inc(xp_psum, 1)
                    ffn2(F, 0)
                if K:
                    level(K, 2)
                if F:
                    ffn1(F, 2)
                    ffn2(F, 1)
                if K:
                    level(K, 3)
                if F:
                    ffn1(F, 3)
                    n, p, _ = F
                    pe.wait_ge(xps_loaded, 16 * 4 * NMU * n)
                    pe.wait_ge(xp_tanh, n)
                    mus(F, 0)
                    ffn2(F, 2)
                if K:
                    level(K, 4)
                if F:
                    ffn1(F, 4)
                    n, p, _ = F
                    pe.wait_ge(yt_ready, NMU * p + 1)
                    mus(F, 1)
                    ffn2(F, 3)
                    pe.wait_ge(yt_ready, NMU * p + 2)
                    pe.wait_ge(y_ready, NMU * p + 1)
                    project(front_ps[:, 0:T], ww1_s, 0).then_inc(w1_psum, 1)
                if K:
                    level(K, 5)
                if F:
                    ffn1(F, 5)
                    n, p, _ = F
                    pe.wait_ge(wt_ready, n)
                    mus(F, 2)
                    ffn2(F, 4)
                if K:
                    level(K, 6)
                if F:
                    n, p, _ = F
                    pe.wait_ge(yt_ready, NMU * p + 3)
                    pe.wait_ge(wst_ready, n)
                    mm(front_ps[:, 0:T], [(ww2_h[:, :], wst[:, :]), (ww2_l[:, :], wst[:, :])])\
                        .then_inc(w2_psum, 1)
                    pe.wait_ge(y_ready, NMU * p + 2)
                    project(front_ps[:, T:2 * T], wr_s, 1).then_inc(r_psum, 1)
                    ffn1(F, 6)
                    ffn2(F, 5)
                    pe.wait_ge(ew_ready, n)
                    pe.wait_ge(r_ready, n)
                    mus(F, 3)
                if K:
                    n, p, _ = K
                    pe.wait_ge(k_upd, L * n)
                    pe.wait_ge(sel_done, L * n)
                    for c in range(C - 1):
                        last = pe.transpose(back_ps[:, c * P:(c + 1) * P],
                                            Kw[:, L % 2, c * P:(c + 1) * P], ident_s[:, :])
                    last.then_inc(kt_psum, 1)
                if F:
                    n, p, _ = F
                    pe.wait_ge(yt_ready, NMU * p + 4)
                    pe.wait_ge(y_ready, NMU * p + 3)
                    project(front_ps[:, 0:T], wk_s, 2).then_inc(k_psum, 1)
                    ffn1(F, 7)
                    ffn2(F, 6)
                if K:
                    n, p, _ = K
                    pe.wait_ge(ktl_ready, n)
                    pe.wait_ge(vl_ready, n)
                    for c in range(C - 1):
                        for h in range(NH):
                            kq = slice(DK * h, DK * h + DK)
                            vq = slice(DV * h, DV * h + DV)
                            last = mm(back_ps[kq, c * DV:(c + 1) * DV],
                                      [(Kth[:, c, kq], vh[:, c, vq]), (Kth[:, c, kq], vl[:, c, vq]),
                                       (Ktl[:, c, kq], vh[:, c, vq])])
                    last.then_inc(u_psum, 1)
                if F:
                    n, p, _ = F
                    pe.wait_ge(k_ready, n)
                    mus(F, 4)
                    ffn2(F, 7)
                if K:
                    n, p, _ = K
                    pe.wait_ge(sxl_ready, n)
                    pe.wait_ge(Rl_ready, n)
                    pe.wait_ge(ph_ready, n)
                    pe.wait_ge(pl_ready, n)
                    for c in range(C):
                        tok = slice(c * P, (c + 1) * P)
                        if c:
                            sh = Sxh[:, c - 1, :, :].rearrange("p h v -> p (h v)")
                            sl = Sxl[:, c - 1, :, :].rearrange("p h v -> p (h v)")
                            mm(back_ps[:, c * VD:(c + 1) * VD],
                               [(Rh[:, tok], sh), (Rh[:, tok], sl), (Rl[:, tok], sh)], stop=False)
                        for h in range(NH):
                            g = slice((c * NH + h) * P, (c * NH + h + 1) * P)
                            vq = slice(DV * h, DV * h + DV)
                            last = mm(back_ps[:, c * VD + DV * h:c * VD + DV * h + DV],
                                      [(Ph[:, g], vh[:, c, vq]), (Ph[:, g], vl[:, c, vq]),
                                       (Pl[:, g], vh[:, c, vq])], start=c == 0, stop=True)
                    last.then_inc(o_psum, 1)
                if F:
                    n, p, _ = F
                    pe.wait_ge(yt_ready, NMU * p + 5)
                    pe.wait_ge(y_ready, NMU * p + 4)
                    for c in range(C):
                        last = mm(front_ps[:, c * VD:(c + 1) * VD],
                                  [(yy[:, 1, a * T + c * P:a * T + (c + 1) * P], wv_s[:, a, :])
                                   for a in range(HB)])
                    last.then_inc(v_psum, 1)
                if K:
                    n, p, _ = K
                    pe.wait_ge(on_ready, n)
                    onf = on[:, :, :].rearrange("p (c h) v -> p c (h v)", c=C)
                    for c in range(C):
                        for a in range(HB):
                            last = pe.transpose(back_ps[:, a * T + c * P:a * T + (c + 1) * P],
                                                onf[:, c, a * P:(a + 1) * P], ident_s[:, :])
                    last.then_inc(oT_psum, 1)
                if F:
                    n, p, _ = F
                    pe.wait_ge(v_ready, n)
                    pe.wait_ge(y_ready, NMU * p + 5)
                    for a in range(HB):
                        last = project(front_ps[:, a * T:(a + 1) * T], wg_s[:, :, a * P:(a + 1) * P], 4)
                    last.then_inc(g_psum, 1)
                if K:
                    n, p, _ = K
                    pe.wait_ge(og_ready, n)
                    for b in range(HB):
                        last = mm(back_ps[:, b * T:(b + 1) * T],
                                  [(wo_s[:, a, b * P:(b + 1) * P], og[:, a, :]) for a in range(HB)])
                    last.then_inc(s_psum, 1)
                    pe.wait_ge(sgt_ready, n)
                    for c in range(C):
                        for a in range(HB):
                            last = pe.transpose(back_ps[:, c * HID + a * P:c * HID + (a + 1) * P],
                                                sgt[:, a, c * P:(c + 1) * P], ident_s[:, :])
                    last.then_inc(outT_psum, 1)

            rows(pe, body)


def _layouts(np, a):
    P_ = 128
    T_, R_, NH_, L_ = 512, 32, 4, 7
    HID_ = a["L0_attn_W_r"].shape[1]

    def cols(v):
        return v.reshape(-1, P_).T

    def lhsT(w):
        return w.T.reshape(-1, P_, w.shape[0]).transpose(1, 0, 2)

    t = np.arange(P_)
    masks = np.zeros((P_, L_, P_ // 2), np.float32)
    for l in range(L_):
        m = 1 << l
        k = np.arange(P_ // 2)
        masks[:, l, :] = (t[:, None] // (2 * m) == k[None, :] // m) & (t[:, None] % (2 * m) < m)
    return {
        "x": a["L0_attn_hidden_states"],
        "mu0": cols(a["L0_attn_mu0"]),
        "wx0": lhsT(a["L0_attn_W_x0"]),
        "wx2": np.tile(a["L0_attn_W_x2"].reshape(HID_, 5, R_).transpose(2, 1, 0), (4, 1, 1)),
        "x_bias": a["L0_attn_x_bias"].reshape(5, -1, P_).transpose(2, 1, 0),
        "wr": lhsT(a["L0_attn_W_r"]),
        "ww1": np.tile(lhsT(a["L0_attn_W_w1"]), (1, 1, 2)),
        "ww2": np.tile(a["L0_attn_W_w2"].T, (2, 1)),
        "b_w2": cols(a["L0_attn_b_w2"]),
        "wk": lhsT(a["L0_attn_W_k"]),
        "wv": lhsT(a["L0_attn_W_v"]),
        "wg": lhsT(a["L0_attn_W_g"]),
        "bonus": a["L0_attn_bonus"].reshape(P_, 1),
        "gn_w": cols(a["L0_attn_gn_weight"]),
        "gn_b": cols(a["L0_attn_gn_bias"]),
        "wo": lhsT(a["L0_attn_W_o"]),
        "w1_rows": a["L0_ffn_w1"].reshape(-1, P_, HID_).transpose(1, 0, 2),
        "w1_cols": lhsT(a["L0_ffn_w1"]).reshape(P_, -1),
        "b1": cols(a["L0_ffn_b1"]),
        "w2_rows": a["L0_ffn_w2"].reshape(-1, P_, a["L0_ffn_w2"].shape[1]).transpose(1, 0, 2),
        "w2_cols": lhsT(a["L0_ffn_w2"]).reshape(P_, -1),
        "b2": cols(a["L0_ffn_b2"]),
        "ident": np.eye(P_, dtype=np.float32),
        "level_masks": masks.reshape(P_, -1),
        "head_ones": (t[:, None] // (P_ // NH_) == np.arange(NH_)[None, :]).astype(np.float32),
    }


def kernel(**inputs):
    import numpy as np
    import concourse.bacc as bacc
    from concourse.bass_utils import run_bass_kernel_spmd

    arrays = {k: np.asarray(v) for k, v in inputs.items()}
    laid = {k: np.ascontiguousarray(v) for k, v in _layouts(np, arrays).items()}
    nc = bacc.Bacc("TRN2", target_bir_lowering=False, num_devices=1)
    args, feed = {}, {}
    for name, a in laid.items():
        feed[f"in_{name}"] = a
        args[name] = nc.dram_tensor(f"in_{name}", a.shape, mybir.dt.from_np(a.dtype), kind="ExternalInput").ap()
    y = nc.dram_tensor("out_y", laid["x"].shape, F32, kind="ExternalOutput").ap()
    rwkv6_gated_ffn(nc, out=y, **args)
    r = run_bass_kernel_spmd(nc, [feed], core_ids=[0])
    return r.results[0]["out_y"]
```

```python
from contextlib import ExitStack

import concourse.bass as bass
from concourse import mybir

ALU = mybir.AluOpType
ACT = mybir.ActivationFunctionType
AX_X = mybir.AxisListType.X
F32 = mybir.dt.float32
F16 = mybir.dt.float16
U8 = mybir.dt.uint8

P = 128
LN_EPS = 1e-5
GN_EPS = 1e-5


def rwkv6_gated_ffn(nc, x, mu0, wx0, wx2, x_bias, wr, ww1, ww2, b_w2, wk, wv, wg, bonus,
                    gn_w, gn_b, wo, w1_rows, w1_cols, b1, w2_rows, w2_cols, b2,
                    ident, level_masks, head_ones, out):
    B, T, HID = x.shape
    HB = HID // P
    C = T // P
    NH = head_ones.shape[1]
    DK = P // NH
    DV = wv.shape[2] // NH
    VD = NH * DV
    NMU = x_bias.shape[2]
    R = wx0.shape[2] // 8
    GLR = ww2.shape[0] // 2
    MT = w1_rows.shape[1]
    L = P.bit_length() - 1
    HALF = P // 2
    DIAG = 4
    CH = C * NH
    MW, MR, MK, MV, MG = 1, 0, 2, 3, 4
    ORDER = (MW, MR, MK, MV, MG)

    with ExitStack() as ctx:
        def sb(name, shape, dt):
            return ctx.enter_context(nc.sbuf_tensor(name, shape, dt))

        def sem(name):
            return ctx.enter_context(nc.semaphore(name))

        front_ps = ctx.enter_context(nc.psum_tensor("front_ps", [P, 2 * 512], F32))
        back_ps = ctx.enter_context(nc.psum_tensor("back_ps", [P, 2 * 512], F32))
        hid_ps = ctx.enter_context(nc.psum_tensor("hid_ps", [P, 2, T], F32))
        ffn_ps = ctx.enter_context(nc.psum_tensor("ffn_ps", [P, HB, T], F32))

        mu0_s = sb("mu0_s", [P, HB], F32)
        wx0_f = sb("wx0_f", [P, HB, 2 * P], F32)
        wx0_h = sb("wx0_h", [P, HB, 2 * P], F16)
        wx0_l = sb("wx0_l", [P, HB, 2 * P], F16)
        wx2_f = sb("wx2_f", [P, NMU, HID], F32)
        wx2_s = sb("wx2_s", [P, NMU, HID], F16)
        xb_s = sb("xb_s", [P, HB, NMU], F32)
        wr_s = sb("wr_s", [P, HB, P], F32)
        wk_s = sb("wk_s", [P, HB, P], F32)
        ww1_s = sb("ww1_s", [P, HB, P], F32)
        ww2_f = sb("ww2_f", [P, P], F32)
        ww2_h = sb("ww2_h", [P, P], F16)
        ww2_l = sb("ww2_l", [P, P], F16)
        bw2_s = sb("bw2_s", [P, 1], F32)
        wv_s = sb("wv_s", [P, HB, VD], F32)
        wv_mean = sb("wv_mean", [P, HB * NH], F32)
        wg_s = sb("wg_s", [P, HB, VD], F32)
        wo_s = sb("wo_s", [P, HB, HID], F32)
        u_s = sb("u_s", [P, 1], F32)
        gnw_s = sb("gnw_s", [P, HB], F32)
        gnb_s = sb("gnb_s", [P, HB], F32)
        b1_s = sb("b1_s", [P, MT], F32)
        b2_s = sb("b2_s", [P, HB], F32)
        alpha1 = sb("alpha1", [P, MT], F32)
        alpha2 = sb("alpha2", [P, HB], F32)
        sign1 = sb("sign1", [P, HB, MT * P], F16)
        sign2 = sb("sign2", [P, MT, HID], F16)
        ident_s = sb("ident_s", [P, P], F32)
        identm_s = sb("identm_s", [P, P], U8)
        masks_s = sb("masks_s", [P, L, HALF], U8)
        ones_s = sb("ones_s", [P, NH], F32)

        xt = sb("xt", [P, C, HID], F32)
        stats = sb("stats", [P, C, 6], F32)
        meanvar = sb("meanvar", [P, C, 2], F32)
        var_eps = sb("var_eps", [P, C], F32)
        rstd = sb("rstd", [P, C], F32)
        minus_half = sb("minus_half", [P, CH], F32)
        xnT = sb("xnT", [P, HB, T + 1], F32)
        xh = sb("xh", [P, HB, T], F16)
        xl = sb("xl", [P, HB, T], F16)
        delta = sb("delta", [P, HB, T], F32)
        y0 = sb("y0", [P, HB, T], F32)
        y0h = sb("y0h", [P, HB, T], F16)
        y0l = sb("y0l", [P, HB, T], F16)
        xpt = sb("xpt", [P, 2, T], F32)
        xph = sb("xph", [P, T], F16)
        xpl = sb("xpl", [P, T], F16)
        xps = sb("xps", [P, NMU, T], F16)
        yt = sb("yt", [P, 2, HB * T], F32)
        yy = sb("yy", [P, 2, HB * T], F32)
        wt = sb("wt", [P, T], F32)
        wst = sb("wst", [P, T], F16)
        ew = sb("ew", [P, T], F32)
        dF = sb("dF", [P, T], F32)
        rkF = sb("rkF", [P, 2, T], F32)
        vF = sb("vF", [P, C, VD], F32)
        tg = sb("tg", [P, HB, T], F32)
        sg = sb("sg", [P, HB, T], F32)
        hf = sb("hf", [P, 2, T], F32)
        hh = sb("hh", [P, 2, T], F16)
        hl = sb("hl", [P, 2, T], F16)
        zh = sb("zh", [P, HB, T], F32)
        gate = sb("gate", [P, HB, T], F32)

        xres = sb("xres", [P, C, HID], F32)
        Rw = sb("Rw", [P, T], F32)
        Kw = sb("Kw", [P, 2, T], F32)
        Dw = [dF] + [sb(f"D{l}", [P, T >> l], F32) for l in range(1, L + 1)]
        zd = sb("zd", [P, T], F32)
        p0 = sb("p0", [P, CH], F32)
        Rx = sb("Rx", [P, 2, CH * HALF], F32)
        PT = sb("PT", [P, CH * P], F32)
        Ph = sb("Ph", [P, CH * P], F16)
        Pl = sb("Pl", [P, CH * P], F16)
        Rh = sb("Rh", [P, T], F16)
        Rl = sb("Rl", [P, T], F16)
        Kth = sb("Kth", [P, C - 1, P], F16)
        Ktl = sb("Ktl", [P, C - 1, P], F16)
        vh = sb("vh", [P, C, VD], F16)
        vl = sb("vl", [P, C, VD], F16)
        St = sb("St", [P, C - 1, DV], F32)
        Sxh = sb("Sxh", [P, C - 1, NH, DV], F16)
        Sxl = sb("Sxl", [P, C - 1, NH, DV], F16)
        on = sb("on", [P, CH, DV], F32)
        ss = sb("ss", [P, CH], F32)
        rs = sb("rs", [P, CH], F32)
        og = sb("og", [P, HB, T], F32)
        sgt = sb("sgt", [P, HB, T], F32)

        w1_rows_s = PT[:, :].rearrange("p (m k) -> p m k", m=MT)
        w1_cols_s = Rx[:, :, :].rearrange("p a b -> p (a b)")
        w2_rows_s = yt[:, :, :]
        masks_f = sgt[:, :, :].rearrange("p a b -> p (a b)")[:, 0:L * HALF]
        w2_cols_s = yy[:, :, :].rearrange("p a b -> p (a b)")

        loads = [(mu0_s, mu0), (wx0_f, wx0), (wx2_f, wx2), (xb_s, x_bias), (wr_s, wr), (wk_s, wk),
                 (ww1_s, ww1), (ww2_f, ww2), (bw2_s, b_w2), (wv_s, wv), (wg_s, wg), (wo_s, wo),
                 (u_s, bonus), (gnw_s, gn_w), (gnb_s, gn_b), (b1_s, b1), (b2_s, b2),
                 (ident_s, ident), (masks_f, level_masks), (ones_s, head_ones)]

        const_loaded = sem("const_loaded")
        ffn_w_loaded = sem("ffn_w_loaded")
        abs_done = sem("abs_done")
        sign_done = sem("sign_done")
        su = sem("su")
        setup_dve = sem("setup_dve")
        setup_pool = sem("setup_pool")

        x_loaded = sem("x_loaded")
        ln_stats = sem("ln_stats")
        ln_aggr = sem("ln_aggr")
        ln_var = sem("ln_var")
        ln_rstd = sem("ln_rstd")
        xn_ready = sem("xn_ready")
        xnT_psum = sem("xnT_psum")
        xnT_ready = sem("xnT_ready")
        xh_ready = sem("xh_ready")
        xl_ready = sem("xl_ready")
        delta_ready = sem("delta_ready")
        y0_ready = sem("y0_ready")
        y0h_ready = sem("y0h_ready")
        y0l_ready = sem("y0l_ready")
        xpw_psum = sem("xpw_psum")
        xpw_tanh = sem("xpw_tanh")
        xpw_high = sem("xpw_high")
        xpw_ready = sem("xpw_ready")
        xp_psum = sem("xp_psum")
        xp_tanh = sem("xp_tanh")
        xph_ready = sem("xph_ready")
        xpl_ready = sem("xpl_ready")
        xps_loaded = {k: sem(f"xps_loaded{k}") for k in (MR, MK, MV, MG)}
        mus_psum = sem("mus_psum")
        yt_ready = sem("yt_ready")
        y_ready = sem("y_ready")
        w1_psum = sem("w1_psum")
        wt_ready = sem("wt_ready")
        wsth_ready = sem("wsth_ready")
        wst_ready = sem("wst_ready")
        w2_psum = sem("w2_psum")
        ew_ready = sem("ew_ready")
        d_ready = sem("d_ready")
        r_psum = sem("r_psum")
        r_ready = sem("r_ready")
        k_psum = sem("k_psum")
        k_ready = sem("k_ready")
        v_psum = sem("v_psum")
        v_ready = sem("v_ready")
        g_psum = sem("g_psum")
        tg_ready = sem("tg_ready")
        sg_ready = sem("sg_ready")
        hid_psum = sem("hid_psum")
        gelu_done = sem("gelu_done")
        hh_ready = sem("hh_ready")
        hl_ready = sem("hl_ready")
        ffn2_done = sem("ffn2_done")
        zh_ready = sem("zh_ready")
        tz_ready = sem("tz_ready")
        gate_ready = sem("gate_ready")
        xres_loaded = sem("xres_loaded")
        rk_taken = sem("rk_taken")
        zd_ready = sem("zd_ready")
        D_ready = sem("D_ready")
        diag_psum = sem("diag_psum")
        p0_ready = sem("p0_ready")
        diag_done = sem("diag_done")
        rx_ready = sem("rx_ready")
        lev_psum = sem("lev_psum")
        sel_done = sem("sel_done")
        r_upd = sem("r_upd")
        k_upd = sem("k_upd")
        vh_ready = sem("vh_ready")
        vl_ready = sem("vl_ready")
        Rh_ready = sem("Rh_ready")
        Rl_ready = sem("Rl_ready")
        kt_psum = sem("kt_psum")
        kth_ready = sem("kth_ready")
        ktl_ready = sem("ktl_ready")
        u_psum = sem("u_psum")
        st_ready = sem("st_ready")
        sxh_ready = sem("sxh_ready")
        sxl_ready = sem("sxl_ready")
        ph_ready = sem("ph_ready")
        pl_ready = sem("pl_ready")
        o_psum = sem("o_psum")
        osq_ready = sem("osq_ready")
        ss_ready = sem("ss_ready")
        ss_eps_ready = sem("ss_eps_ready")
        rs_ready = sem("rs_ready")
        on_ready = sem("on_ready")
        oT_psum = sem("oT_psum")
        oT_ready = sem("oT_ready")
        og_ready = sem("og_ready")
        s_psum = sem("s_psum")
        sgt_ready = sem("sgt_ready")
        outT_psum = sem("outT_psum")
        out_ready = sem("out_ready")
        stored = sem("stored")

        x_tok = x.rearrange("b (c p) h -> b p c h", p=P)
        out_tok = out.rearrange("b (c p) h -> b p c h", p=P)

        def wait(eng, s, value):
            if not (isinstance(value, int) and value <= 0):
                eng.wait_ge(s, value)

        def blocks(ap, half, m):
            return ap.rearrange("p (b two m) -> p b two m", two=2, m=m)[:, :, half, :]

        def rows(eng, body):
            body((1, 0, 0), None, None)
            body((2, 1, 1), (1, 0, 0), None)
            body((3, 2, 2), (2, 1, 1), (1, 0, 0))
            with eng.Fori(2, B - 1) as i:
                before = eng.snap(i - 1)
                here = eng.snap(i + 0)
                after = eng.snap(i + 1)
                last = eng.snap(i + 2)
                body((last, after, after), (after, here, here), (here, before, before))
            body(None, (B, B - 1, B - 1), (B - 1, B - 2, B - 2))
            body(None, None, (B, B - 1, B - 1))

        def do(step, row, *args):
            if row:
                step(*row, *args)

        block = ctx.enter_context(nc.Block())

        @block.sync
        def _(sp):
            for dst, src in loads:
                sp.dma_start(dst if dst is masks_f else dst[:], src).then_inc(const_loaded, 16)

            def load_x(n, p, i):
                wait(sp, xnT_psum, p)
                sp.dma_start(xt[:, :, :], x_tok[i]).then_inc(x_loaded, 16)

            def load_residual(n, p, j):
                wait(sp, stored, 16 * p)
                sp.dma_start(xres[:, :, :], x_tok[j]).then_inc(xres_loaded, 16)

            def stack(n, p, _):
                sp.wait_ge(xpl_ready, n)
                wait(sp, sg_ready, p)
                for row, k in enumerate((MR, MK, MV, MG)):
                    for q in range(4):
                        part = (xph, xph, xpl, xpl)[q]
                        sp.dma_start(xps[R * q:R * q + R, k, :], part[R * row:R * row + R, :])\
                            .then_inc(xps_loaded[k], 16)

            def store(n, p, j):
                sp.wait_ge(out_ready, n)
                sp.dma_start(out_tok[j], xres[:, :, :]).then_inc(stored, 16)

            def body(A, F, K):
                do(load_x, A)
                do(stack, F)
                do(load_residual, K)
                do(store, K)

            rows(sp, body)
            sp.wait_ge(stored, 16 * B)

        @block.scalar
        def _(act):
            act.dma_start(w1_rows_s, w1_rows).then_inc(ffn_w_loaded, 16)
            act.dma_start(w2_rows_s, w2_rows).then_inc(ffn_w_loaded, 16)
            act.dma_start(w1_cols_s, w1_cols).then_inc(ffn_w_loaded, 16)
            act.dma_start(w2_cols_s, w2_cols).then_inc(ffn_w_loaded, 16)
            act.wait_ge(ffn_w_loaded, 64)
            act.activation(w1_rows_s, w1_rows_s, ACT.Abs).then_inc(abs_done, 1)
            act.activation(w2_rows_s, w2_rows_s, ACT.Abs).then_inc(abs_done, 1)
            act.activation(sign1[:, :, :].rearrange("p a b -> p (a b)"), w1_cols_s, ACT.Sign)
            act.activation(sign2[:, :, :].rearrange("p a b -> p (a b)"), w2_cols_s, ACT.Sign)\
                .then_inc(sign_done, 1)
            act.wait_ge(setup_dve, 1)
            act.wait_ge(setup_pool, 1)
            front_halves = front_ps[:, :].rearrange("p (a t) -> p a t", a=HB)
            hid_halves = hid_ps[:, :, :]

            def x_channels(n, p, _):
                act.wait_ge(xnT_psum, n)
                wait(act, y_ready, NMU * p)
                act.activation(xnT[:, :, 1:T + 1], hid_halves, ACT.Copy).then_inc(xnT_ready, 1)
                wait(act, hid_psum, MT * p)
                act.activation(xh[:, :, :], hid_halves, ACT.Copy).then_inc(xh_ready, 1)

            def gelu(n, p, _, m):
                act.wait_ge(hid_psum, MT * p + m + 1)
                wait(act, hl_ready, MT * p + max(m - 1, 0))
                act.activation(hf[:, m % 2, :], hid_ps[:, m % 2, :], ACT.Gelu, bias=b1_s[:, m:m + 1],
                               scale=alpha1[:, m:m + 1]).then_inc(gelu_done, 1)

            def expand(n, p, _, l):
                m = 1 << l
                if l:
                    act.wait_ge(r_upd, L * p + l)
                else:
                    act.wait_ge(rk_taken, n)
                wait(act, lev_psum, L * p + max(l - 1, 0))
                for h in range(NH):
                    q = slice(DK * h, DK * h + DK)
                    src = Rw[q, :].rearrange("p (c b two m) -> p c b two m", c=C, two=2, m=m)[:, :, :, 1, :]
                    dst = Rx[q, l % 2, :].rearrange("p (c h b m) -> p c h b m", c=C, h=NH, m=m)[:, :, h, :, :]
                    last = act.activation(dst, src, ACT.Copy)
                last.then_inc(rx_ready, 1)

            def mix_tanh(n, p, _):
                act.wait_ge(xpw_psum, n)
                wait(act, xpw_ready, p)
                act.activation(xpt[:, 0, :], front_ps[:, 0:T], ACT.Tanh).then_inc(xpw_tanh, 1)
                act.wait_ge(xp_psum, n)
                wait(act, xpl_ready, p)
                act.activation(xpt[:, 1, :], front_ps[:, T:2 * T], ACT.Tanh).then_inc(xp_tanh, 1)

            def w_tanh(n, p, _):
                act.wait_ge(w1_psum, n)
                wait(act, wst_ready, p)
                act.activation(wt[:, :], front_ps[:, 0:T], ACT.Tanh).then_inc(wt_ready, 1)

            def decay(n, p, _):
                act.wait_ge(w2_psum, n)
                act.activation(ew[:, :], front_ps[:, 0:T], ACT.Exp, bias=bw2_s[:, 0:1])\
                    .then_inc(ew_ready, 1)
                act.wait_ge(ew_ready, n)
                wait(act, k_upd, L * (p - 1) + 1)
                wait(act, r_upd, L * (p - 1) + 1)
                wait(act, D_ready, L * (p - 1) + 1)
                act.activation(dF[:, :], ew[:, :], ACT.Exp, scale=-1.0).then_inc(d_ready, 1)

            def r_out(n, p, _):
                act.wait_ge(r_psum, n)
                wait(act, zd_ready, p)
                act.activation(rkF[:, 0, :], front_ps[:, T:2 * T], ACT.Copy).then_inc(r_ready, 1)

            def k_out(n, p, _):
                act.wait_ge(k_psum, n)
                act.activation(rkF[:, 1, :], front_ps[:, 0:T], ACT.Copy).then_inc(k_ready, 1)

            def v_out(n, p, _):
                act.wait_ge(v_psum, n)
                wait(act, vl_ready, p)
                act.activation(vF[:, :, :].rearrange("p a b -> p (a b)"), front_ps[:, :], ACT.Copy)\
                    .then_inc(v_ready, 1)

            def g_tanh(n, p, _):
                act.wait_ge(g_psum, n)
                wait(act, sg_ready, p)
                act.activation(tg[:, :, :], front_halves, ACT.Tanh, scale=0.5).then_inc(tg_ready, 1)

            def scores_high(n, p, _):
                act.wait_ge(sel_done, L * n)
                act.wait_ge(diag_done, n)
                wait(act, o_psum, p)
                act.activation(Ph[:, :], PT[:, :], ACT.Copy).then_inc(ph_ready, 1)

            def o_square(n, p, _):
                act.wait_ge(o_psum, n)
                wait(act, oT_psum, p)
                act.activation(on[:, :, :].rearrange("p a b -> p (a b)"), back_ps[:, :], ACT.Square)\
                    .then_inc(osq_ready, 1)

            def o_affine(n, p, _):
                act.wait_ge(oT_psum, n)
                wait(act, s_psum, p)
                for a in range(HB):
                    last = act.activation(og[:, a, :], back_ps[:, a * T:(a + 1) * T], ACT.Identity,
                                          bias=gnb_s[:, a:a + 1], scale=gnw_s[:, a:a + 1])
                last.then_inc(oT_ready, 1)

            def gate_tanh(n, p, _):
                act.wait_ge(ffn2_done, MT * n)
                wait(act, gate_ready, p)
                for a in range(HB):
                    last = act.activation(zh[:, a, :], ffn_ps[:, a, :], ACT.Identity,
                                          bias=b2_s[:, a:a + 1], scale=alpha2[:, a:a + 1])
                last.then_inc(zh_ready, 1)
                act.wait_ge(zh_ready, n)
                wait(act, sgt_ready, p)
                act.activation(gate[:, :, :], zh[:, :, :], ACT.Tanh).then_inc(tz_ready, 1)

            def body(A, F, K):
                do(r_out, F)
                do(expand, K, 6)
                do(gelu, F, 4)
                do(scores_high, K)
                do(gelu, F, 5)
                do(k_out, F)
                do(gelu, F, 6)
                do(gelu, F, 7)
                do(o_square, K)
                do(x_channels, A)
                do(v_out, F)
                do(o_affine, K)
                do(g_tanh, F)
                do(gate_tanh, F)
                do(mix_tanh, A)
                do(gelu, A, 0)
                do(gelu, A, 1)
                do(expand, F, 0)
                do(expand, F, 1)
                do(gelu, A, 2)
                do(expand, F, 2)
                do(w_tanh, A)
                do(expand, F, 3)
                do(gelu, A, 3)
                do(expand, F, 4)
                do(expand, F, 5)
                do(decay, A)

            rows(act, body)

        @block.gpsimd
        def _(pool):
            pool.memset(Sxh[:, :, :, :], 0.0)
            pool.memset(Sxl[:, :, :, :], 0.0)
            pool.memset(xnT[:, :, 0:1], 0.0)
            pool.memset(minus_half[:, :], -0.5)
            pool.wait_ge(abs_done, 2)
            pool.wait_ge(sign_done, 1)
            pool.memset(Rx[:, :, :], 0.0)
            pool.wait_ge(setup_dve, 1)
            pool.memset(PT[:, :], 0.0).then_inc(setup_pool, 1)

            def k_step(n, p, _, l):
                m = 1 << l
                if l:
                    pool.wait_ge(k_upd, L * p + l)
                    pool.wait_ge(D_ready, L * p + l)
                    pool.wait_ge(lev_psum, L * p + l)
                else:
                    pool.wait_ge(rk_taken, n)
                    pool.wait_ge(d_ready, n)
                    wait(pool, kt_psum, p)
                src, dst = Kw[:, l % 2, :], Kw[:, (l + 1) % 2, :]
                D2 = Dw[l][:, :].rearrange("p (b two) -> p b two", two=2)[:, :, 1:2]\
                    .to_broadcast([P, T // (2 * m), m])
                pool.tensor_tensor(blocks(dst, 0, m), blocks(src, 0, m), D2, ALU.mult)
                pool.tensor_copy(blocks(dst, 1, m), blocks(src, 1, m)).then_inc(k_upd, 1)

            def h_low(n, p, _, m):
                pool.wait_ge(hh_ready, MT * p + m + 1)
                wait(pool, ffn2_done, MT * p + max(m - 1, 0))
                pool.tensor_tensor(hl[:, m % 2, :], hf[:, m % 2, :], hh[:, m % 2, :], ALU.subtract)\
                    .then_inc(hl_ready, 1)

            def mix_sum(n, p, _, o):
                pool.wait_ge(yt_ready, NMU * p + o + 1)
                used = (w1_psum, r_psum, k_psum, v_psum, g_psum)
                wait(pool, used[o - 2], n) if o >= 2 else wait(pool, used[4 - o], p)
                pool.tensor_tensor(yy[:, o % 2, :].rearrange("p (a t) -> p a t", a=HB),
                                   yt[:, o % 2, :].rearrange("p (a t) -> p a t", a=HB),
                                   xnT[:, :, 1:T + 1], ALU.add).then_inc(y_ready, 1)

            def ln_power(n, p, _):
                pool.wait_ge(ln_var, n)
                wait(pool, xn_ready, p)
                pool.tensor_tensor(rstd[:, :], var_eps[:, :], minus_half[:, 0:C], ALU.pow)\
                    .then_inc(ln_rstd, 1)

            def x_low(n, p, _):
                pool.wait_ge(xnT_ready, n)
                pool.wait_ge(xh_ready, n)
                pool.tensor_tensor(xl[:, :, :], xnT[:, :, 1:T + 1], xh[:, :, :], ALU.subtract)\
                    .then_inc(xl_ready, 1)

            def o_power(n, p, _):
                pool.wait_ge(ss_eps_ready, n)
                wait(pool, on_ready, p)
                pool.tensor_tensor(rs[:, :], ss[:, :], minus_half[:, :], ALU.pow)\
                    .then_inc(rs_ready, 1)

            def body(A, F, K):
                do(h_low, K, 7)
                do(k_step, K, 0)
                do(h_low, F, 0)
                do(mix_sum, F, 0)
                do(mix_sum, F, 1)
                do(k_step, K, 1)
                do(h_low, F, 1)
                do(k_step, K, 2)
                do(ln_power, A)
                do(k_step, K, 3)
                do(mix_sum, F, 2)
                do(k_step, K, 4)
                do(k_step, K, 5)
                do(h_low, F, 2)
                do(k_step, K, 6)
                do(h_low, F, 3)
                do(h_low, F, 4)
                do(h_low, F, 5)
                do(mix_sum, F, 3)
                do(mix_sum, F, 4)
                do(h_low, F, 6)
                do(o_power, K)
                do(x_low, A)

            rows(pool, body)

        @block.vector
        def _(dve):
            step = [0]

            def then(ins):
                step[0] += 1
                ins.then_inc(su, 1)
                dve.wait_ge(su, step[0])

            dve.wait_ge(const_loaded, 16 * len(loads))
            dve.tensor_copy(identm_s[:, :], ident_s[:, :])
            dve.tensor_copy(masks_s[:, :, :].rearrange("p l t -> p (l t)"), masks_f)
            then(dve.tensor_copy(wx0_h[:, :, :], wx0_f[:, :, :]))
            dve.tensor_tensor(wx0_l[:, :, :], wx0_f[:, :, :], wx0_h[:, :, :], ALU.subtract)
            then(dve.tensor_copy(wx2_s[:, :, :], wx2_f[:, :, :]))
            for q in (1, 3):
                s = slice(R * q, R * q + R)
                dve.tensor_tensor(wx2_s[s, :, :], wx2_f[s, :, :], wx2_s[s, :, :], ALU.subtract)
            then(dve.tensor_copy(ww2_h[:, :], ww2_f[:, :]))
            dve.tensor_tensor(ww2_l[:, :], ww2_f[:, :], ww2_h[:, :], ALU.subtract)
            wv_heads = wv_s[:, :, :].rearrange("p a (h v) -> p (a h) v", v=DV)
            then(dve.tensor_reduce(wv_mean[:, :], wv_heads, AX_X, ALU.add))
            then(dve.tensor_scalar(wv_mean[:, :], wv_mean[:, :], 1.0 / DV, None, ALU.mult))
            dve.tensor_tensor(wv_heads, wv_heads,
                              wv_mean[:, :].unsqueeze(2).to_broadcast([P, HB * NH, DV]), ALU.subtract)
            dve.tensor_scalar(gnw_s[:, :], gnw_s[:, :], 0.5 * DV ** 0.5, None, ALU.mult)
            dve.tensor_scalar(gnb_s[:, :], gnb_s[:, :], 0.5, None, ALU.mult)
            dve.tensor_scalar(b2_s[:, :], b2_s[:, :], 0.5, None, ALU.mult)
            dve.wait_ge(abs_done, 2)
            then(dve.tensor_reduce(alpha1[:, :], w1_rows_s, AX_X, ALU.add))
            dve.tensor_scalar(alpha1[:, :], alpha1[:, :], 1.0 / HID, None, ALU.mult)
            then(dve.tensor_reduce(alpha2[:, :], w2_rows_s, AX_X, ALU.add))
            dve.tensor_scalar(alpha2[:, :], alpha2[:, :], 0.5 / (MT * P), None, ALU.mult)\
                .then_inc(setup_dve, 1)
            dve.wait_ge(setup_dve, 1)
            dve.wait_ge(setup_pool, 1)

            def ln_stats_step(n, p, _):
                dve.wait_ge(x_loaded, 16 * n)
                for c in range(C):
                    last = dve.bn_stats(stats[:, c, :], xt[:, c, :])
                last.then_inc(ln_stats, 1)
                dve.wait_ge(setup_dve, 1)
                dve.wait_ge(ln_stats, n)
                for c in range(C):
                    last = dve.bn_aggr(meanvar[:, c, :], stats[:, c, :])
                last.then_inc(ln_aggr, 1)
                dve.wait_ge(ln_aggr, n)
                wait(dve, ln_rstd, p)
                dve.tensor_scalar(var_eps[:, :], meanvar[:, :, 1], LN_EPS, None, ALU.add)\
                    .then_inc(ln_var, 1)

            def ln_apply(n, p, _):
                dve.wait_ge(ln_rstd, n)
                for c in range(C):
                    last = dve.tensor_scalar(xt[:, c, :], xt[:, c, :], meanvar[:, c, 0:1],
                                             rstd[:, c:c + 1], ALU.subtract, ALU.mult)
                last.then_inc(xn_ready, 1)

            def shift(n, p, _):
                dve.wait_ge(xnT_ready, n)
                dve.tensor_tensor(delta[:, :, :], xnT[:, :, 0:T], xnT[:, :, 1:T + 1], ALU.subtract)\
                    .then_inc(delta_ready, 1)
                dve.wait_ge(delta_ready, n)
                for a in range(HB):
                    last = dve.scalar_tensor_tensor(y0[:, a, :], delta[:, a, :], mu0_s[:, a:a + 1],
                                                    xnT[:, a, 1:T + 1], ALU.mult, ALU.add)
                last.then_inc(y0_ready, 1)
                dve.wait_ge(y0_ready, n)
                wait(dve, xp_psum, p)
                dve.tensor_copy(y0h[:, :, :], y0[:, :, :]).then_inc(y0h_ready, 1)
                dve.wait_ge(y0h_ready, n)
                dve.tensor_tensor(y0l[:, :, :], y0[:, :, :], y0h[:, :, :], ALU.subtract)\
                    .then_inc(y0l_ready, 1)

            def split_xpw(n, p, _):
                dve.wait_ge(xpw_tanh, n)
                wait(dve, mus_psum, NMU * (p - 1) + 1)
                dve.tensor_copy(xps[:, MW, :], xpt[:, 0, :]).then_inc(xpw_high, 1)
                dve.wait_ge(xpw_high, n)
                low = slice(2 * R, 4 * R)
                dve.tensor_tensor(xps[low, MW, :], xpt[low, 0, :], xps[low, MW, :], ALU.subtract)\
                    .then_inc(xpw_ready, 1)

            def split_xp(n, p, _):
                dve.wait_ge(xp_tanh, n)
                for k in (MR, MK, MV, MG):
                    wait(dve, xps_loaded[k], 64 * p)
                dve.tensor_copy(xph[:, :], xpt[:, 1, :]).then_inc(xph_ready, 1)
                dve.wait_ge(xph_ready, n)
                dve.tensor_tensor(xpl[:, :], xpt[:, 1, :], xph[:, :], ALU.subtract)\
                    .then_inc(xpl_ready, 1)

            def mix(n, p, _, o):
                k = ORDER[o]
                dve.wait_ge(mus_psum, NMU * p + o + 1)
                wait(dve, y_ready, NMU * p + max(o - 1, 0))
                for a in range(HB):
                    last = dve.scalar_tensor_tensor(yt[:, o % 2, a * T:(a + 1) * T],
                                                    front_ps[:, a * T:(a + 1) * T], xb_s[:, a, k:k + 1],
                                                    delta[:, a, :], ALU.add, ALU.mult)
                last.then_inc(yt_ready, 1)

            def split_w(n, p, _):
                dve.wait_ge(wt_ready, n)
                wait(dve, w2_psum, p)
                dve.tensor_copy(wst[:, :], wt[:, :]).then_inc(wsth_ready, 1)
                dve.wait_ge(wsth_ready, n)
                dve.tensor_tensor(wst[GLR:P, :], wt[GLR:P, :], wst[GLR:P, :], ALU.subtract)\
                    .then_inc(wst_ready, 1)

            def h_high(n, p, _, m):
                dve.wait_ge(gelu_done, MT * p + m + 1)
                wait(dve, ffn2_done, MT * p + max(m - 1, 0))
                dve.tensor_copy(hh[:, m % 2, :], hf[:, m % 2, :]).then_inc(hh_ready, 1)

            def g_silu(n, p, _):
                dve.wait_ge(tg_ready, n)
                wait(dve, og_ready, p)
                dve.scalar_tensor_tensor(sg[:, :, :], tg[:, :, :], 1.0,
                                         front_ps[:, :].rearrange("p (a t) -> p a t", a=HB),
                                         ALU.add, ALU.mult).then_inc(sg_ready, 1)

            def z_silu(n, p, _):
                dve.wait_ge(tz_ready, n)
                dve.scalar_tensor_tensor(gate[:, :, :], gate[:, :, :], 1.0, zh[:, :, :],
                                         ALU.add, ALU.mult).then_inc(gate_ready, 1)

            def take(n, p, _):
                dve.wait_ge(r_ready, n)
                dve.wait_ge(k_ready, n)
                wait(dve, Rl_ready, p)
                dve.tensor_copy(Rw[:, :], rkF[:, 0, :])
                wait(dve, lev_psum, L * p)
                dve.tensor_copy(Kw[:, 0, :], rkF[:, 1, :]).then_inc(rk_taken, 1)
                wait(dve, diag_psum, p)
                dve.scalar_tensor_tensor(zd[:, :], rkF[:, 0, :], u_s[:, 0:1], rkF[:, 1, :],
                                         ALU.mult, ALU.mult).then_inc(zd_ready, 1)

            def decays(n, p, _, levels):
                for l in levels:
                    pair = Dw[l - 1][:, :].rearrange("p (b two) -> p b two", two=2)
                    if l > 1:
                        dve.wait_ge(D_ready, L * p + l - 1)
                    else:
                        dve.wait_ge(d_ready, n)
                        wait(dve, k_upd, L * p)
                    dve.tensor_tensor(Dw[l][:, :], pair[:, :, 0], pair[:, :, 1], ALU.mult)\
                        .then_inc(D_ready, 1)

            def diagonal_out(n, p, _):
                dve.wait_ge(diag_psum, n)
                wait(dve, diag_done, p)
                dve.tensor_copy(p0[:, :], back_ps[:, 0:CH]).then_inc(p0_ready, 1)

            def diagonal(n, p, _):
                dve.wait_ge(setup_dve, 1)
                dve.wait_ge(p0_ready, n)
                dve.wait_ge(sel_done, L * p + DIAG)
                dve.copy_predicated(PT[:, :].rearrange("p (g t) -> p g t", g=CH),
                                    identm_s[:, :].unsqueeze(1).to_broadcast([P, CH, P]),
                                    p0[:, :].unsqueeze(2).to_broadcast([P, CH, P]))\
                    .then_inc(diag_done, 1)

            def select(n, p, _, l):
                m = 1 << l
                dve.wait_ge(setup_dve, 1)
                dve.wait_ge(lev_psum, L * p + l + 1)
                if l == 0:
                    wait(dve, ph_ready, p)
                    wait(dve, pl_ready, p)
                elif l == DIAG:
                    dve.wait_ge(diag_done, n)
                dst = PT[:, :].rearrange("p (g b two m) -> p g b two m", g=CH, two=2, m=m)[:, :, :, 1, :]
                src = back_ps[:, :].rearrange("p (g b m) -> p g b m", g=CH, m=m)
                msk = masks_s[:, l, :].rearrange("p (b m) -> p b m", m=m).unsqueeze(1)\
                    .to_broadcast([P, CH, HALF // m, m])
                dve.copy_predicated(dst, msk, src).then_inc(sel_done, 1)

            def r_step(n, p, _, l):
                m = 1 << l
                dve.wait_ge(rx_ready, L * p + l + 1)
                if l:
                    dve.wait_ge(D_ready, L * p + l)
                    dve.wait_ge(r_upd, L * p + l)
                D1 = Dw[l][:, :].rearrange("p (b two) -> p b two", two=2)[:, :, 0:1]\
                    .to_broadcast([P, T // (2 * m), m])
                dve.tensor_tensor(blocks(Rw[:, :], 1, m), blocks(Rw[:, :], 1, m), D1, ALU.mult)\
                    .then_inc(r_upd, 1)

            def split_v(n, p, _):
                dve.wait_ge(v_ready, n)
                wait(dve, o_psum, p)
                dve.tensor_copy(vh[:, :, :], vF[:, :, :]).then_inc(vh_ready, 1)
                dve.wait_ge(vh_ready, n)
                dve.tensor_tensor(vl[:, :, :], vF[:, :, :], vh[:, :, :], ALU.subtract)\
                    .then_inc(vl_ready, 1)

            def split_r(n, p, _):
                dve.wait_ge(r_upd, L * n)
                wait(dve, o_psum, p)
                dve.tensor_copy(Rh[:, :], Rw[:, :]).then_inc(Rh_ready, 1)
                dve.wait_ge(Rh_ready, n)
                dve.tensor_tensor(Rl[:, :], Rw[:, :], Rh[:, :], ALU.subtract).then_inc(Rl_ready, 1)

            def split_kt(n, p, _):
                dve.wait_ge(kt_psum, n)
                wait(dve, u_psum, p)
                kt_ps = back_ps[:, 0:(C - 1) * P].rearrange("p (c k) -> p c k", c=C - 1)
                dve.tensor_copy(Kth[:, :, :], kt_ps).then_inc(kth_ready, 1)
                dve.wait_ge(kth_ready, n)
                dve.tensor_tensor(Ktl[:, :, :], kt_ps, Kth[:, :, :], ALU.subtract)\
                    .then_inc(ktl_ready, 1)

            def scores_low(n, p, _):
                dve.wait_ge(ph_ready, n)
                dve.tensor_tensor(Pl[:, :], PT[:, :], Ph[:, :], ALU.subtract).then_inc(pl_ready, 1)

            def states(n, p, _):
                dve.wait_ge(u_psum, n)
                wait(dve, sxl_ready, p)
                dve.tensor_copy(St[:, 0, :], back_ps[:, 0:DV]).then_inc(st_ready, 1)
                for c in range(1, C - 1):
                    dve.wait_ge(st_ready, (C - 1) * p + c)
                    dve.scalar_tensor_tensor(St[:, c, :], St[:, c - 1, :], Dw[L][:, c:c + 1],
                                             back_ps[:, c * DV:(c + 1) * DV], ALU.mult, ALU.add)\
                        .then_inc(st_ready, 1)
                dve.wait_ge(st_ready, (C - 1) * n)
                for h in range(NH):
                    q = slice(DK * h, DK * h + DK)
                    last = dve.tensor_copy(Sxh[q, :, h, :], St[q, :, :])
                last.then_inc(sxh_ready, 1)
                dve.wait_ge(sxh_ready, n)
                for h in range(NH):
                    q = slice(DK * h, DK * h + DK)
                    last = dve.tensor_tensor(Sxl[q, :, h, :], St[q, :, :], Sxh[q, :, h, :],
                                             ALU.subtract)
                last.then_inc(sxl_ready, 1)

            def o_variance(n, p, _):
                dve.wait_ge(osq_ready, n)
                dve.tensor_reduce(ss[:, :], on[:, :, :], AX_X, ALU.add).then_inc(ss_ready, 1)
                dve.wait_ge(ss_ready, n)
                dve.tensor_scalar(ss[:, :], ss[:, :], DV * GN_EPS, None, ALU.add)\
                    .then_inc(ss_eps_ready, 1)

            def o_normalise(n, p, _):
                dve.wait_ge(rs_ready, n)
                dve.tensor_tensor(on[:, :, :], back_ps[:, :].rearrange("p (g v) -> p g v", v=DV),
                                  rs[:, :].unsqueeze(2).to_broadcast([P, CH, DV]), ALU.mult)\
                    .then_inc(on_ready, 1)

            def o_gate(n, p, _):
                dve.wait_ge(oT_ready, n)
                dve.wait_ge(sg_ready, n)
                dve.tensor_tensor(og[:, :, :], og[:, :, :], sg[:, :, :], ALU.mult)\
                    .then_inc(og_ready, 1)

            def s_gate(n, p, _):
                dve.wait_ge(s_psum, n)
                dve.wait_ge(gate_ready, n)
                wait(dve, outT_psum, p)
                dve.tensor_tensor(sgt[:, :, :], back_ps[:, :].rearrange("p (a t) -> p a t", a=HB),
                                  gate[:, :, :], ALU.mult).then_inc(sgt_ready, 1)

            def residual(n, p, _):
                dve.wait_ge(outT_psum, n)
                dve.wait_ge(xres_loaded, 16 * n)
                dve.tensor_tensor(xres[:, :, :], back_ps[:, :].rearrange("p (c h) -> p c h", c=C),
                                  xres[:, :, :], ALU.add).then_inc(out_ready, 1)

            def body(A, F, K):
                do(r_step, K, 1)
                do(select, K, 0)
                do(mix, F, 1)
                do(ln_stats_step, A)
                do(r_step, K, 2)
                do(split_w, F)
                do(select, K, 1)
                do(h_high, F, 2)
                do(r_step, K, 3)
                do(mix, F, 2)
                do(select, K, 2)
                do(ln_apply, A)
                do(h_high, F, 3)
                do(r_step, K, 4)
                do(select, K, 3)
                do(diagonal, K)
                do(select, K, 4)
                do(r_step, K, 5)
                do(mix, F, 3)
                do(r_step, K, 6)
                do(select, K, 5)
                do(split_v, K)
                do(select, K, 6)
                do(split_r, K)
                do(split_kt, K)
                do(h_high, F, 4)
                do(scores_low, K)
                do(h_high, F, 5)
                do(states, K)
                do(mix, F, 4)
                do(decays, F, range(1, 4))
                do(h_high, F, 6)
                do(o_variance, K)
                do(shift, A)
                do(o_normalise, K)
                do(h_high, F, 7)
                do(o_gate, K)
                do(g_silu, F)
                do(decays, F, range(4, L + 1))
                do(s_gate, K)
                do(split_xpw, A)
                do(split_xp, A)
                do(residual, K)
                do(take, F)
                do(z_silu, F)
                do(diagonal_out, F)
                do(h_high, A, 0)
                do(h_high, A, 1)
                do(r_step, F, 0)
                do(mix, A, 0)

            rows(dve, body)

        @block.tensor
        def _(pe):
            pe.wait_ge(setup_dve, 1)
            pe.wait_ge(setup_pool, 1)
            pe.wait_ge(sign_done, 1)

            def mm(dst, pairs, start=True, stop=True):
                for k, (a, b) in enumerate(pairs):
                    last = pe.matmul(dst, a, b, start=start and k == 0, stop=stop and k == len(pairs) - 1,
                                     skip_group_check=True)
                return last

            def x_transpose(n, p, _):
                pe.wait_ge(xn_ready, n)
                wait(pe, gelu_done, MT * p)
                for c in range(C):
                    for a in range(HB):
                        last = pe.transpose(hid_ps[:, a, c * P:(c + 1) * P],
                                            xt[:, c, a * P:(a + 1) * P], ident_s[:, :])
                last.then_inc(xnT_psum, 1)

            def mix_rank(n, p, _):
                pe.wait_ge(y0l_ready, n)
                wait(pe, sg_ready, p)
                for k, done in ((0, xpw_psum), (1, xp_psum)):
                    cols = slice(k * P, (k + 1) * P)
                    mm(front_ps[:, k * T:(k + 1) * T],
                       [(w[:, a, cols], y[:, a, :]) for a in range(HB)
                        for w, y in ((wx0_h, y0h), (wx0_l, y0h), (wx0_h, y0l))]).then_inc(done, 1)

            def ffn1(n, p, _, m):
                if m == 0:
                    pe.wait_ge(xh_ready, n)
                    pe.wait_ge(xl_ready, n)
                wait(pe, gelu_done, MT * p + max(m - 1, 0))
                mm(hid_ps[:, m % 2, :], [(sign1[:, a, m * P:(m + 1) * P], part[:, a, :])
                                         for a in range(HB) for part in (xh, xl)]).then_inc(hid_psum, 1)

            def ffn2(n, p, _, m):
                if m == 0:
                    wait(pe, zh_ready, p)
                pe.wait_ge(hh_ready, MT * p + m + 1)
                pe.wait_ge(hl_ready, MT * p + m + 1)
                for a in range(HB):
                    last = mm(ffn_ps[:, a, :], [(sign2[:, m, a * P:(a + 1) * P], part[:, m % 2, :])
                                                for part in (hh, hl)], start=m == 0, stop=m == MT - 1)
                last.then_inc(ffn2_done, 1)

            def mus(n, p, _, o):
                k = ORDER[o]
                if o == 0:
                    pe.wait_ge(xpw_ready, n)
                    pe.wait_ge(xp_tanh, n)
                else:
                    pe.wait_ge(xps_loaded[k], 64 * n)
                if o == 1:
                    pe.wait_ge(yt_ready, NMU * p + 1)
                if o == 2:
                    pe.wait_ge(wt_ready, n)
                    pe.wait_ge(yt_ready, NMU * p + 2)
                if o == 3:
                    pe.wait_ge(ew_ready, n)
                    pe.wait_ge(r_ready, n)
                if o == 4:
                    pe.wait_ge(k_ready, n)
                for a in range(HB):
                    last = mm(front_ps[:, a * T:(a + 1) * T], [(wx2_s[:, k, a * P:(a + 1) * P], xps[:, k, :])])
                last.then_inc(mus_psum, 1)

            def project(dst, w, o):
                return mm(dst, [(w[:, a, :], yy[:, o % 2, a * T:(a + 1) * T]) for a in range(HB)])

            def w_rank(n, p, _):
                pe.wait_ge(yt_ready, NMU * p + 2)
                pe.wait_ge(y_ready, NMU * p + 1)
                project(front_ps[:, 0:T], ww1_s, 0).then_inc(w1_psum, 1)

            def w_proj(n, p, _):
                pe.wait_ge(yt_ready, NMU * p + 3)
                pe.wait_ge(wst_ready, n)
                mm(front_ps[:, 0:T], [(ww2_h[:, :], wst[:, :]), (ww2_l[:, :], wst[:, :])])\
                    .then_inc(w2_psum, 1)

            def r_proj(n, p, _):
                pe.wait_ge(y_ready, NMU * p + 2)
                project(front_ps[:, T:2 * T], wr_s, 1).then_inc(r_psum, 1)

            def k_proj(n, p, _):
                pe.wait_ge(yt_ready, NMU * p + 4)
                pe.wait_ge(y_ready, NMU * p + 3)
                project(front_ps[:, 0:T], wk_s, 2).then_inc(k_psum, 1)

            def v_proj(n, p, _):
                pe.wait_ge(yt_ready, NMU * p + 5)
                pe.wait_ge(y_ready, NMU * p + 4)
                for c in range(C):
                    last = mm(front_ps[:, c * VD:(c + 1) * VD],
                              [(yy[:, 1, a * T + c * P:a * T + (c + 1) * P], wv_s[:, a, :])
                               for a in range(HB)])
                last.then_inc(v_psum, 1)

            def g_proj(n, p, _):
                pe.wait_ge(v_ready, n)
                pe.wait_ge(y_ready, NMU * p + 5)
                for a in range(HB):
                    last = project(front_ps[:, a * T:(a + 1) * T], wg_s[:, :, a * P:(a + 1) * P], 4)
                last.then_inc(g_psum, 1)

            def diagonal(n, p, _):
                pe.wait_ge(zd_ready, n)
                wait(pe, out_ready, p)
                for c in range(C):
                    last = mm(back_ps[:, c * NH:(c + 1) * NH], [(zd[:, c * P:(c + 1) * P], ones_s[:, :])])
                last.then_inc(diag_psum, 1)

            def level(n, p, _, l):
                pe.wait_ge(rx_ready, L * p + l + 1)
                if l:
                    pe.wait_ge(k_upd, L * p + l)
                    pe.wait_ge(sel_done, L * p + l)
                else:
                    pe.wait_ge(rk_taken, n)
                    pe.wait_ge(p0_ready, n)
                for c in range(C):
                    last = mm(back_ps[:, c * NH * HALF:(c + 1) * NH * HALF],
                              [(Kw[:, l % 2, c * P:(c + 1) * P],
                                Rx[:, l % 2, c * NH * HALF:(c + 1) * NH * HALF])])
                last.then_inc(lev_psum, 1)

            def k_transpose(n, p, _):
                pe.wait_ge(k_upd, L * n)
                pe.wait_ge(sel_done, L * n)
                for c in range(C - 1):
                    last = pe.transpose(back_ps[:, c * P:(c + 1) * P],
                                        Kw[:, L % 2, c * P:(c + 1) * P], ident_s[:, :])
                last.then_inc(kt_psum, 1)

            def updates(n, p, _):
                pe.wait_ge(ktl_ready, n)
                pe.wait_ge(vl_ready, n)
                for c in range(C - 1):
                    for h in range(NH):
                        kq = slice(DK * h, DK * h + DK)
                        vq = slice(DV * h, DV * h + DV)
                        last = mm(back_ps[kq, c * DV:(c + 1) * DV],
                                  [(Kth[:, c, kq], vh[:, c, vq]), (Kth[:, c, kq], vl[:, c, vq]),
                                   (Ktl[:, c, kq], vh[:, c, vq])])
                last.then_inc(u_psum, 1)

            def attend(n, p, _):
                pe.wait_ge(sxl_ready, n)
                pe.wait_ge(Rl_ready, n)
                pe.wait_ge(ph_ready, n)
                pe.wait_ge(pl_ready, n)
                for c in range(C):
                    tok = slice(c * P, (c + 1) * P)
                    if c:
                        sh = Sxh[:, c - 1, :, :].rearrange("p h v -> p (h v)")
                        sl = Sxl[:, c - 1, :, :].rearrange("p h v -> p (h v)")
                        mm(back_ps[:, c * VD:(c + 1) * VD],
                           [(Rh[:, tok], sh), (Rh[:, tok], sl), (Rl[:, tok], sh)], stop=False)
                    for h in range(NH):
                        g = slice((c * NH + h) * P, (c * NH + h + 1) * P)
                        vq = slice(DV * h, DV * h + DV)
                        last = mm(back_ps[:, c * VD + DV * h:c * VD + DV * h + DV],
                                  [(Ph[:, g], vh[:, c, vq]), (Ph[:, g], vl[:, c, vq]),
                                   (Pl[:, g], vh[:, c, vq])], start=c == 0, stop=True)
                last.then_inc(o_psum, 1)

            def o_transpose(n, p, _):
                pe.wait_ge(on_ready, n)
                onf = on[:, :, :].rearrange("p (c h) v -> p c (h v)", c=C)
                for c in range(C):
                    for a in range(HB):
                        last = pe.transpose(back_ps[:, a * T + c * P:a * T + (c + 1) * P],
                                            onf[:, c, a * P:(a + 1) * P], ident_s[:, :])
                last.then_inc(oT_psum, 1)

            def o_proj(n, p, _):
                pe.wait_ge(og_ready, n)
                for b in range(HB):
                    last = mm(back_ps[:, b * T:(b + 1) * T],
                              [(wo_s[:, a, b * P:(b + 1) * P], og[:, a, :]) for a in range(HB)])
                last.then_inc(s_psum, 1)

            def s_transpose(n, p, _):
                pe.wait_ge(sgt_ready, n)
                for c in range(C):
                    for a in range(HB):
                        last = pe.transpose(back_ps[:, c * HID + a * P:c * HID + (a + 1) * P],
                                            sgt[:, a, c * P:(c + 1) * P], ident_s[:, :])
                last.then_inc(outT_psum, 1)

            def body(A, F, K):
                do(level, K, 3)
                do(r_proj, F)
                do(level, K, 4)
                do(ffn1, F, 5)
                do(mus, F, 3)
                do(level, K, 5)
                do(ffn2, F, 2)
                do(level, K, 6)
                do(ffn2, F, 3)
                do(k_transpose, K)
                do(k_proj, F)
                do(updates, K)
                do(ffn1, F, 6)
                do(mus, F, 4)
                do(ffn1, F, 7)
                do(ffn2, F, 4)
                do(x_transpose, A)
                do(attend, K)
                do(v_proj, F)
                do(ffn2, F, 5)
                do(g_proj, F)
                do(o_transpose, K)
                do(ffn2, F, 6)
                do(ffn2, F, 7)
                do(o_proj, K)
                do(mix_rank, A)
                do(s_transpose, K)
                do(ffn1, A, 0)
                do(ffn1, A, 1)
                do(mus, A, 0)
                do(ffn1, A, 2)
                do(diagonal, F)
                do(ffn1, A, 3)
                do(level, F, 0)
                do(mus, A, 1)
                do(ffn2, A, 0)
                do(w_rank, A)
                do(level, F, 1)
                do(ffn1, A, 4)
                do(mus, A, 2)
                do(level, F, 2)
                do(ffn2, A, 1)
                do(w_proj, A)

            rows(pe, body)


def _layouts(np, a):
    P_ = 128
    T_, R_, NH_, L_ = 512, 32, 4, 7
    HID_ = a["L0_attn_W_r"].shape[1]

    def cols(v):
        return v.reshape(-1, P_).T

    def lhsT(w):
        return w.T.reshape(-1, P_, w.shape[0]).transpose(1, 0, 2)

    t = np.arange(P_)
    masks = np.zeros((P_, L_, P_ // 2), np.float32)
    for l in range(L_):
        m = 1 << l
        k = np.arange(P_ // 2)
        masks[:, l, :] = (t[:, None] // (2 * m) == k[None, :] // m) & (t[:, None] % (2 * m) < m)
    return {
        "x": a["L0_attn_hidden_states"],
        "mu0": cols(a["L0_attn_mu0"]),
        "wx0": lhsT(a["L0_attn_W_x0"].reshape(5, R_, HID_)[[1, 1, 1, 1, 0, 2, 3, 4]].reshape(-1, HID_)),
        "wx2": np.tile(a["L0_attn_W_x2"].reshape(HID_, 5, R_).transpose(2, 1, 0), (4, 1, 1)),
        "x_bias": a["L0_attn_x_bias"].reshape(5, -1, P_).transpose(2, 1, 0),
        "wr": lhsT(a["L0_attn_W_r"]),
        "ww1": np.tile(lhsT(a["L0_attn_W_w1"]), (1, 1, 2)),
        "ww2": np.tile(a["L0_attn_W_w2"].T, (2, 1)),
        "b_w2": cols(a["L0_attn_b_w2"]),
        "wk": lhsT(a["L0_attn_W_k"]),
        "wv": lhsT(a["L0_attn_W_v"]),
        "wg": lhsT(a["L0_attn_W_g"]),
        "bonus": a["L0_attn_bonus"].reshape(P_, 1),
        "gn_w": cols(a["L0_attn_gn_weight"]),
        "gn_b": cols(a["L0_attn_gn_bias"]),
        "wo": lhsT(a["L0_attn_W_o"]),
        "w1_rows": a["L0_ffn_w1"].reshape(-1, P_, HID_).transpose(1, 0, 2),
        "w1_cols": lhsT(a["L0_ffn_w1"]).reshape(P_, -1),
        "b1": cols(a["L0_ffn_b1"]),
        "w2_rows": a["L0_ffn_w2"].reshape(-1, P_, a["L0_ffn_w2"].shape[1]).transpose(1, 0, 2),
        "w2_cols": lhsT(a["L0_ffn_w2"]).reshape(P_, -1),
        "b2": cols(a["L0_ffn_b2"]),
        "ident": np.eye(P_, dtype=np.float32),
        "level_masks": masks.reshape(P_, -1),
        "head_ones": (t[:, None] // (P_ // NH_) == np.arange(NH_)[None, :]).astype(np.float32),
    }


def kernel(**inputs):
    import numpy as np
    import concourse.bacc as bacc
    from concourse.bass_utils import run_bass_kernel_spmd

    arrays = {k: np.asarray(v) for k, v in inputs.items()}
    laid = {k: np.ascontiguousarray(v) for k, v in _layouts(np, arrays).items()}
    nc = bacc.Bacc("TRN2", target_bir_lowering=False, num_devices=1)
    args, feed = {}, {}
    for name, a in laid.items():
        feed[f"in_{name}"] = a
        args[name] = nc.dram_tensor(f"in_{name}", a.shape, mybir.dt.from_np(a.dtype), kind="ExternalInput").ap()
    y = nc.dram_tensor("out_y", laid["x"].shape, F32, kind="ExternalOutput").ap()
    rwkv6_gated_ffn(nc, out=y, **args)
    r = run_bass_kernel_spmd(nc, [feed], core_ids=[0])
    return r.results[0]["out_y"]
```

```python
from contextlib import ExitStack

import concourse.bass as bass
from concourse import mybir

ALU = mybir.AluOpType
ACT = mybir.ActivationFunctionType
AX_X = mybir.AxisListType.X
F32 = mybir.dt.float32
F16 = mybir.dt.float16
U8 = mybir.dt.uint8

P = 128
LN_EPS = 1e-5
GN_EPS = 1e-5


def rwkv6_gated_ffn(nc, x, mu0, wx0, wx2, x_bias, wr, ww1, ww2, b_w2, wk, wv, wg, bonus,
                    gn_w, gn_b, wo, w1_rows, w1_cols, b1, w2_rows, w2_cols, b2,
                    ident, level_masks, head_ones, out):
    B, T, HID = x.shape
    HB = HID // P
    C = T // P
    NH = head_ones.shape[1]
    DK = P // NH
    DV = wv.shape[2] // NH
    VD = NH * DV
    NMU = x_bias.shape[2]
    R = wx0.shape[2] // 8
    GLR = ww2.shape[0] // 2
    MT = w1_rows.shape[1]
    L = P.bit_length() - 1
    HALF = P // 2
    CH = C * NH
    HC = C // 2
    HT = HC * P
    HG = HC * NH
    BANK = 512
    MW, MR, MK, MV, MG = 1, 0, 2, 3, 4
    ORDER = (MW, MR, MK, MV, MG)

    with ExitStack() as ctx:
        def sb(name, shape, dt):
            return ctx.enter_context(nc.sbuf_tensor(name, shape, dt))

        def sem(name):
            return ctx.enter_context(nc.semaphore(name))

        front_ps = ctx.enter_context(nc.psum_tensor("front_ps", [P, 2 * 512], F32))
        back_ps = ctx.enter_context(nc.psum_tensor("back_ps", [P, 2 * 512], F32))
        hid_ps = ctx.enter_context(nc.psum_tensor("hid_ps", [P, 2, T], F32))
        ffn_ps = ctx.enter_context(nc.psum_tensor("ffn_ps", [P, HB, T], F32))

        mu0_s = sb("mu0_s", [P, HB], F32)
        wx0_f = sb("wx0_f", [P, HB, 2 * P], F32)
        wx0_h = sb("wx0_h", [P, HB, 2 * P], F16)
        wx0_l = sb("wx0_l", [P, HB, 2 * P], F16)
        wx2_f = sb("wx2_f", [P, NMU, HID], F32)
        wx2_s = sb("wx2_s", [P, NMU, HID], F16)
        xb_s = sb("xb_s", [P, HB, NMU], F32)
        wr_s = sb("wr_s", [P, HB, P], F32)
        wk_s = sb("wk_s", [P, HB, P], F32)
        ww1_s = sb("ww1_s", [P, HB, P], F32)
        ww2_f = sb("ww2_f", [P, P], F32)
        ww2_h = sb("ww2_h", [P, P], F16)
        ww2_l = sb("ww2_l", [P, P], F16)
        bw2_s = sb("bw2_s", [P, 1], F32)
        wv_s = sb("wv_s", [P, HB, VD], F32)
        wv_mean = sb("wv_mean", [P, HB * NH], F32)
        wg_s = sb("wg_s", [P, HB, VD], F32)
        wo_s = sb("wo_s", [P, HB, HID], F32)
        u_s = sb("u_s", [P, 1], F32)
        gnw_s = sb("gnw_s", [P, HB], F32)
        gnb_s = sb("gnb_s", [P, HB], F32)
        b1_s = sb("b1_s", [P, MT], F32)
        b2_s = sb("b2_s", [P, HB], F32)
        alpha1 = sb("alpha1", [P, MT], F32)
        alpha2 = sb("alpha2", [P, HB], F32)
        sign1 = sb("sign1", [P, HB, MT * P], F16)
        sign2 = sb("sign2", [P, MT, HID], F16)
        ident_s = sb("ident_s", [P, P], F32)
        masks_s = sb("masks_s", [P, L, HALF], U8)
        ones_s = sb("ones_s", [P, NH], F32)

        xt = sb("xt", [P, C, HID], F32)
        stats = sb("stats", [P, C, 6], F32)
        meanvar = sb("meanvar", [P, C, 2], F32)
        var_eps = sb("var_eps", [P, C], F32)
        rstd = sb("rstd", [P, C], F32)
        minus_half = sb("minus_half", [P, CH], F32)
        xnT = sb("xnT", [P, HB, T + 1], F32)
        xh = sb("xh", [P, HB, T], F16)
        xl = sb("xl", [P, HB, T], F16)
        delta = sb("delta", [P, HB, T], F32)
        y0 = sb("y0", [P, HB, T], F32)
        y0h = sb("y0h", [P, HB, T], F16)
        y0l = sb("y0l", [P, HB, T], F16)
        xpt = sb("xpt", [P, 2, T], F32)
        xph = sb("xph", [P, T], F16)
        xpl = sb("xpl", [P, T], F16)
        xps = sb("xps", [P, NMU, T], F16)
        yt = sb("yt", [P, 2, HB * T], F32)
        yy = sb("yy", [P, 2, HB * T], F32)
        wt = sb("wt", [P, T], F32)
        wst = sb("wst", [P, T], F16)
        ew = sb("ew", [P, T], F32)
        dF = sb("dF", [P, T], F32)
        rkF = sb("rkF", [P, 2, T], F32)
        tg = sb("tg", [P, HB, T], F32)
        sg = sb("sg", [P, HB, T], F32)
        hf = sb("hf", [P, 2, T], F32)
        hh = sb("hh", [P, 2, T], F16)
        hl = sb("hl", [P, 2, T], F16)
        zh = sb("zh", [P, HB, T], F32)
        gate = sb("gate", [P, HB, T], F32)

        xres = sb("xres", [P, C, HID], F32)
        Rw = sb("Rw", [P, T], F32)
        Kw = sb("Kw", [P, T], F32)
        Dw = [dF] + [sb(f"D{l}", [P, T >> l], F32) for l in range(1, L + 1)]
        zd = sb("zd", [P, T], F32)
        p0 = sb("p0", [P, CH], F32)
        Rx = sb("Rx", [P, 2, CH * HALF], F32)
        PT = sb("PT", [P, CH * P], F32)
        Ph = sb("Ph", [P, CH * P], F16)
        Pl = sb("Pl", [P, CH * P], F16)
        Rh = sb("Rh", [P, T], F16)
        Rl = sb("Rl", [P, T], F16)
        Kth = sb("Kth", [P, C - 1, P], F16)
        Ktl = sb("Ktl", [P, C - 1, P], F16)
        vh = sb("vh", [P, C, VD], F16)
        vl = sb("vl", [P, C, VD], F16)
        St = sb("St", [P, C - 1, DV], F32)
        Sxh = sb("Sxh", [P, C - 1, NH, DV], F16)
        Sxl = sb("Sxl", [P, C - 1, NH, DV], F16)
        on = sb("on", [P, CH, DV], F32)
        ss = sb("ss", [P, CH], F32)
        rs = sb("rs", [P, CH], F32)
        og = sb("og", [P, HB, T], F32)
        sgt = sb("sgt", [P, HB, T], F32)

        w1_rows_s = PT[:, :].rearrange("p (m k) -> p m k", m=MT)
        w1_cols_s = Rx[:, :, :].rearrange("p a b -> p (a b)")
        w2_rows_s = yt[:, :, :]
        masks_f = sgt[:, :, :].rearrange("p a b -> p (a b)")[:, 0:L * HALF]
        w2_cols_s = yy[:, :, :].rearrange("p a b -> p (a b)")

        loads = [(mu0_s, mu0), (wx0_f, wx0), (wx2_f, wx2), (xb_s, x_bias), (wr_s, wr), (wk_s, wk),
                 (ww1_s, ww1), (ww2_f, ww2), (bw2_s, b_w2), (wv_s, wv), (wg_s, wg), (wo_s, wo),
                 (u_s, bonus), (gnw_s, gn_w), (gnb_s, gn_b), (b1_s, b1), (b2_s, b2),
                 (ident_s, ident), (masks_f, level_masks), (ones_s, head_ones)]

        const_loaded = sem("const_loaded")
        ffn_w_loaded = sem("ffn_w_loaded")
        abs_done = sem("abs_done")
        sign_done = sem("sign_done")
        su = sem("su")
        setup_dve = sem("setup_dve")
        setup_pool = sem("setup_pool")

        x_loaded = sem("x_loaded")
        ln_stats = sem("ln_stats")
        ln_aggr = sem("ln_aggr")
        ln_var = sem("ln_var")
        ln_rstd = sem("ln_rstd")
        xn_ready = sem("xn_ready")
        xnT_psum = sem("xnT_psum")
        xnT_ready = sem("xnT_ready")
        xh_ready = sem("xh_ready")
        xl_ready = sem("xl_ready")
        delta_ready = sem("delta_ready")
        y0_ready = sem("y0_ready")
        y0h_ready = sem("y0h_ready")
        y0l_ready = sem("y0l_ready")
        xpw_psum = sem("xpw_psum")
        xpw_tanh = sem("xpw_tanh")
        xpw_high = sem("xpw_high")
        xpw_ready = sem("xpw_ready")
        xp_psum = sem("xp_psum")
        xp_tanh = sem("xp_tanh")
        xph_ready = sem("xph_ready")
        xpl_ready = sem("xpl_ready")
        xps_loaded = {k: sem(f"xps_loaded{k}") for k in (MR, MK, MV, MG)}
        mus_psum = sem("mus_psum")
        yt_ready = sem("yt_ready")
        y_ready = sem("y_ready")
        w1_psum = sem("w1_psum")
        wt_ready = sem("wt_ready")
        wsth_ready = sem("wsth_ready")
        wst_ready = sem("wst_ready")
        w2_psum = sem("w2_psum")
        ew_ready = sem("ew_ready")
        d_ready = sem("d_ready")
        r_psum = sem("r_psum")
        r_ready = sem("r_ready")
        k_psum = sem("k_psum")
        k_ready = sem("k_ready")
        v_psum = sem("v_psum")
        g_psum = sem("g_psum")
        tg_ready = sem("tg_ready")
        sg_ready = sem("sg_ready")
        hid_psum = sem("hid_psum")
        gelu_done = sem("gelu_done")
        hh_ready = sem("hh_ready")
        hl_ready = sem("hl_ready")
        ffn2_done = sem("ffn2_done")
        zh_ready = sem("zh_ready")
        tz_ready = sem("tz_ready")
        gate_ready = sem("gate_ready")
        xres_loaded = sem("xres_loaded")
        rk_taken = sem("rk_taken")
        zd_ready = sem("zd_ready")
        D_ready = sem("D_ready")
        diag_psum = sem("diag_psum")
        p0_ready = sem("p0_ready")
        diag_done = [sem(f"diag_done{b}") for b in range(2)]
        rx_ready = sem("rx_ready")
        lev_psum = [sem(f"lev_psum{b}") for b in range(2)]
        sel_done = [sem(f"sel_done{b}") for b in range(2)]
        r_upd = sem("r_upd")
        k_upd = sem("k_upd")
        vh_ready = sem("vh_ready")
        vl_ready = sem("vl_ready")
        Rh_ready = sem("Rh_ready")
        Rl_ready = sem("Rl_ready")
        kt_psum = sem("kt_psum")
        kth_ready = sem("kth_ready")
        ktl_ready = sem("ktl_ready")
        u_psum = sem("u_psum")
        st_ready = sem("st_ready")
        sxh_ready = sem("sxh_ready")
        sxl_ready = sem("sxl_ready")
        ph_ready = [sem(f"ph_ready{b}") for b in range(2)]
        pl_ready = [sem(f"pl_ready{b}") for b in range(2)]
        o_psum = [sem(f"o_psum{b}") for b in range(2)]
        osq_ready = [sem(f"osq_ready{b}") for b in range(2)]
        ss_ready = [sem(f"ss_ready{b}") for b in range(2)]
        ss_eps_ready = [sem(f"ss_eps_ready{b}") for b in range(2)]
        rs_ready = [sem(f"rs_ready{b}") for b in range(2)]
        on_ready = [sem(f"on_ready{b}") for b in range(2)]
        oT_psum = [sem(f"oT_psum{b}") for b in range(2)]
        oT_ready = [sem(f"oT_ready{b}") for b in range(2)]
        og_ready = [sem(f"og_ready{b}") for b in range(2)]
        s_psum = [sem(f"s_psum{b}") for b in range(2)]
        sgt_ready = [sem(f"sgt_ready{b}") for b in range(2)]
        outT_psum = [sem(f"outT_psum{b}") for b in range(2)]
        out_ready = [sem(f"out_ready{b}") for b in range(2)]
        stored = sem("stored")

        x_tok = x.rearrange("b (c p) h -> b p c h", p=P)
        out_tok = out.rearrange("b (c p) h -> b p c h", p=P)

        def wait(eng, s, value):
            if not (isinstance(value, int) and value <= 0):
                eng.wait_ge(s, value)

        def blocks(ap, half, m):
            return ap.rearrange("p (b two m) -> p b two m", two=2, m=m)[:, :, half, :]

        def rows(eng, body):
            body((1, 0, 0), None, None)
            body((2, 1, 1), (1, 0, 0), None)
            body((3, 2, 2), (2, 1, 1), (1, 0, 0))
            with eng.Fori(2, B - 1) as i:
                before = eng.snap(i - 1)
                here = eng.snap(i + 0)
                after = eng.snap(i + 1)
                last = eng.snap(i + 2)
                body((last, after, after), (after, here, here), (here, before, before))
            body(None, (B, B - 1, B - 1), (B - 1, B - 2, B - 2))
            body(None, None, (B, B - 1, B - 1))

        def do(step, row, *args):
            if row:
                step(*row, *args)

        block = ctx.enter_context(nc.Block())

        @block.sync
        def _(sp):
            for dst, src in loads:
                sp.dma_start(dst if dst is masks_f else dst[:], src).then_inc(const_loaded, 16)

            def load_x(n, p, i):
                wait(sp, xnT_psum, p)
                sp.dma_start(xt[:, :, :], x_tok[i]).then_inc(x_loaded, 16)

            def load_residual(n, p, j):
                wait(sp, stored, 16 * p)
                sp.dma_start(xres[:, :, :], x_tok[j]).then_inc(xres_loaded, 16)

            def stack(n, p, _):
                sp.wait_ge(xpl_ready, n)
                wait(sp, sg_ready, p)
                for row, k in enumerate((MR, MK, MV, MG)):
                    for q in range(4):
                        part = (xph, xph, xpl, xpl)[q]
                        sp.dma_start(xps[R * q:R * q + R, k, :], part[R * row:R * row + R, :])\
                            .then_inc(xps_loaded[k], 16)

            def store(n, p, j):
                for b in range(2):
                    sp.wait_ge(out_ready[b], n)
                sp.dma_start(out_tok[j], xres[:, :, :]).then_inc(stored, 16)

            def body(A, F, K):
                do(load_x, A)
                do(stack, F)
                do(load_residual, K)
                do(store, K)

            rows(sp, body)
            sp.wait_ge(stored, 16 * B)

        @block.scalar
        def _(act):
            act.dma_start(w1_rows_s, w1_rows).then_inc(ffn_w_loaded, 16)
            act.dma_start(w2_rows_s, w2_rows).then_inc(ffn_w_loaded, 16)
            act.dma_start(w1_cols_s, w1_cols).then_inc(ffn_w_loaded, 16)
            act.dma_start(w2_cols_s, w2_cols).then_inc(ffn_w_loaded, 16)
            act.wait_ge(ffn_w_loaded, 64)
            act.activation(w1_rows_s, w1_rows_s, ACT.Abs).then_inc(abs_done, 1)
            act.activation(w2_rows_s, w2_rows_s, ACT.Abs).then_inc(abs_done, 1)
            act.activation(sign1[:, :, :].rearrange("p a b -> p (a b)"), w1_cols_s, ACT.Sign)
            act.activation(sign2[:, :, :].rearrange("p a b -> p (a b)"), w2_cols_s, ACT.Sign)\
                .then_inc(sign_done, 1)
            act.wait_ge(setup_dve, 1)
            act.wait_ge(setup_pool, 1)
            front_halves = front_ps[:, :].rearrange("p (a t) -> p a t", a=HB)
            hid_halves = hid_ps[:, :, :]

            def x_channels(n, p, _):
                act.wait_ge(xnT_psum, n)
                wait(act, y_ready, NMU * p)
                act.activation(xnT[:, :, 1:T + 1], hid_halves, ACT.Copy).then_inc(xnT_ready, 1)
                wait(act, hid_psum, MT * p)
                act.activation(xh[:, :, :], hid_halves, ACT.Copy).then_inc(xh_ready, 1)

            def gelu(n, p, _, m):
                act.wait_ge(hid_psum, MT * p + m + 1)
                wait(act, ffn2_done, MT * p + max(m - 1, 0))
                wait(act, hl_ready, MT * p + max(m - 1, 0))
                for dst, done in ((hh, hh_ready), (hf, gelu_done)):
                    act.activation(dst[:, m % 2, :], hid_ps[:, m % 2, :], ACT.Gelu,
                                   bias=b1_s[:, m:m + 1], scale=alpha1[:, m:m + 1]).then_inc(done, 1)

            def expand(n, p, _, l):
                m = 1 << l
                if l:
                    act.wait_ge(r_upd, L * p + l)
                else:
                    act.wait_ge(rk_taken, n)
                wait(act, lev_psum[1], L * p + max(l - 1, 0))
                for h in range(NH):
                    q = slice(DK * h, DK * h + DK)
                    src = Rw[q, :].rearrange("p (c b two m) -> p c b two m", c=C, two=2, m=m)[:, :, :, 1, :]
                    dst = Rx[q, l % 2, :].rearrange("p (c h b m) -> p c h b m", c=C, h=NH, m=m)[:, :, h, :, :]
                    last = act.activation(dst, src, ACT.Copy)
                last.then_inc(rx_ready, 1)

            def mix_tanh(n, p, _):
                act.wait_ge(xpw_psum, n)
                wait(act, mus_psum, NMU * (p - 1) + 1)
                act.activation(xps[:, MW, :], front_ps[:, 0:T], ACT.Tanh).then_inc(xpw_high, 1)
                wait(act, xpw_ready, p)
                act.activation(xpt[:, 0, :], front_ps[:, 0:T], ACT.Tanh).then_inc(xpw_tanh, 1)
                act.wait_ge(xp_psum, n)
                for k in (MR, MK, MV, MG):
                    wait(act, xps_loaded[k], 64 * p)
                act.activation(xph[:, :], front_ps[:, T:2 * T], ACT.Tanh).then_inc(xph_ready, 1)
                wait(act, xpl_ready, p)
                act.activation(xpt[:, 1, :], front_ps[:, T:2 * T], ACT.Tanh).then_inc(xp_tanh, 1)

            def y0_high(n, p, _):
                act.wait_ge(y0_ready, n)
                wait(act, xp_psum, p)
                act.activation(y0h[:, :, :], y0[:, :, :], ACT.Copy).then_inc(y0h_ready, 1)

            def w_tanh(n, p, _):
                act.wait_ge(w1_psum, n)
                wait(act, w2_psum, p)
                act.activation(wst[:, :], front_ps[:, 0:T], ACT.Tanh).then_inc(wsth_ready, 1)
                wait(act, wst_ready, p)
                act.activation(wt[:, :], front_ps[:, 0:T], ACT.Tanh).then_inc(wt_ready, 1)

            def decay(n, p, _):
                act.wait_ge(w2_psum, n)
                act.activation(ew[:, :], front_ps[:, 0:T], ACT.Exp, bias=bw2_s[:, 0:1])\
                    .then_inc(ew_ready, 1)
                act.wait_ge(ew_ready, n)
                wait(act, k_upd, L * (p - 1) + 1)
                wait(act, r_upd, L * (p - 1) + 1)
                wait(act, D_ready, L * (p - 1) + 1)
                act.activation(dF[:, :], ew[:, :], ACT.Exp, scale=-1.0).then_inc(d_ready, 1)

            def r_out(n, p, _):
                act.wait_ge(r_psum, n)
                wait(act, zd_ready, p)
                act.activation(rkF[:, 0, :], front_ps[:, T:2 * T], ACT.Copy).then_inc(r_ready, 1)

            def k_out(n, p, _):
                act.wait_ge(k_psum, n)
                act.activation(rkF[:, 1, :], front_ps[:, 0:T], ACT.Copy).then_inc(k_ready, 1)

            def v_out(n, p, _):
                act.wait_ge(v_psum, n)
                wait(act, o_psum[1], p)
                act.activation(vh[:, :, :].rearrange("p a b -> p (a b)"), front_ps[:, :], ACT.Copy)\
                    .then_inc(vh_ready, 1)

            def g_tanh(n, p, _):
                act.wait_ge(g_psum, n)
                wait(act, sg_ready, p)
                act.activation(tg[:, :, :], front_halves, ACT.Tanh, scale=0.5).then_inc(tg_ready, 1)

            def scores_high(n, p, _, b):
                act.wait_ge(sel_done[b], L * n)
                wait(act, o_psum[b], p)
                half = slice(b * HG * P, (b + 1) * HG * P)
                act.activation(Ph[:, half], PT[:, half], ACT.Copy).then_inc(ph_ready[b], 1)

            def kt_high(n, p, _):
                act.wait_ge(kt_psum, n)
                wait(act, u_psum, p)
                act.activation(Kth[:, :, :], back_ps[:, BANK:BANK + (C - 1) * P]
                               .rearrange("p (c k) -> p c k", c=C - 1), ACT.Copy).then_inc(kth_ready, 1)

            def o_square(n, p, _, b):
                act.wait_ge(o_psum[b], n)
                wait(act, oT_psum[b], p)
                act.activation(on[:, b * HG:(b + 1) * HG, :].rearrange("p a b -> p (a b)"),
                               back_ps[:, b * BANK:(b + 1) * BANK], ACT.Square).then_inc(osq_ready[b], 1)

            def o_affine(n, p, _, b):
                act.wait_ge(oT_psum[b], n)
                wait(act, s_psum[b], p)
                for a in range(HB):
                    src = back_ps[:, b * BANK + a * HT:b * BANK + (a + 1) * HT]
                    last = act.activation(og[:, a, b * HT:(b + 1) * HT], src, ACT.Identity,
                                          bias=gnb_s[:, a:a + 1], scale=gnw_s[:, a:a + 1])
                last.then_inc(oT_ready[b], 1)

            def gate_tanh(n, p, _):
                act.wait_ge(ffn2_done, MT * n)
                wait(act, gate_ready, p)
                for a in range(HB):
                    last = act.activation(zh[:, a, :], ffn_ps[:, a, :], ACT.Identity,
                                          bias=b2_s[:, a:a + 1], scale=alpha2[:, a:a + 1])
                last.then_inc(zh_ready, 1)
                act.wait_ge(zh_ready, n)
                for b in range(2):
                    wait(act, sgt_ready[b], p)
                act.activation(gate[:, :, :], zh[:, :, :], ACT.Tanh).then_inc(tz_ready, 1)

            def body(A, F, K):
                do(expand, K, 2)
                do(w_tanh, F)
                do(expand, K, 3)
                do(expand, K, 4)
                do(expand, K, 5)
                do(decay, F)
                do(r_out, F)
                do(expand, K, 6)
                do(gelu, F, 5)
                do(k_out, F)
                do(gelu, F, 6)
                do(scores_high, K, 0)
                do(kt_high, K)
                do(gelu, F, 7)
                do(scores_high, K, 1)
                do(x_channels, A)
                do(o_square, K, 0)
                do(v_out, F)
                do(o_square, K, 1)
                do(y0_high, A)
                do(expand, F, 0)
                do(o_affine, K, 1)
                do(o_affine, K, 0)
                do(g_tanh, F)
                do(gate_tanh, F)
                do(gelu, A, 0)
                do(gelu, A, 1)
                do(mix_tanh, A)
                do(gelu, A, 2)
                do(expand, F, 1)
                do(gelu, A, 3)
                do(gelu, A, 4)

            rows(act, body)

        @block.gpsimd
        def _(pool):
            pool.memset(Sxh[:, :, :, :], 0.0)
            pool.memset(Sxl[:, :, :, :], 0.0)
            pool.memset(xnT[:, :, 0:1], 0.0)
            pool.memset(minus_half[:, :], -0.5)
            pool.wait_ge(abs_done, 2)
            pool.wait_ge(sign_done, 1)
            pool.memset(Rx[:, :, :], 0.0)
            pool.wait_ge(setup_dve, 1)
            pool.memset(PT[:, :], 0.0).then_inc(setup_pool, 1)

            def k_step(n, p, _, l):
                m = 1 << l
                pool.wait_ge(lev_psum[1], L * p + l + 1)
                if l:
                    pool.wait_ge(k_upd, L * p + l)
                    pool.wait_ge(D_ready, L * p + l)
                else:
                    pool.wait_ge(rk_taken, n)
                    pool.wait_ge(d_ready, n)
                D2 = Dw[l][:, :].rearrange("p (b two) -> p b two", two=2)[:, :, 1:2]\
                    .to_broadcast([P, T // (2 * m), m])
                pool.tensor_tensor(blocks(Kw[:, :], 0, m), blocks(Kw[:, :], 0, m), D2, ALU.mult)\
                    .then_inc(k_upd, 1)

            def h_low(n, p, _, m):
                pool.wait_ge(gelu_done, MT * p + m + 1)
                wait(pool, ffn2_done, MT * p + max(m - 1, 0))
                pool.tensor_tensor(hl[:, m % 2, :], hf[:, m % 2, :], hh[:, m % 2, :], ALU.subtract)\
                    .then_inc(hl_ready, 1)

            def mix_sum(n, p, _, o):
                pool.wait_ge(yt_ready, NMU * p + o + 1)
                used = (w1_psum, r_psum, k_psum, v_psum, g_psum)
                wait(pool, used[o - 2], n) if o >= 2 else wait(pool, used[4 - o], p)
                pool.tensor_tensor(yy[:, o % 2, :].rearrange("p (a t) -> p a t", a=HB),
                                   yt[:, o % 2, :].rearrange("p (a t) -> p a t", a=HB),
                                   xnT[:, :, 1:T + 1], ALU.add).then_inc(y_ready, 1)

            def ln_power(n, p, _):
                pool.wait_ge(ln_var, n)
                wait(pool, xn_ready, p)
                pool.tensor_tensor(rstd[:, :], var_eps[:, :], minus_half[:, 0:C], ALU.pow)\
                    .then_inc(ln_rstd, 1)

            def diagonal_in(n, p, _, b):
                pool.wait_ge(p0_ready, n)
                wait(pool, ph_ready[b], p)
                wait(pool, pl_ready[b], p)
                pool.tensor_tensor(PT[:, b * HG * P:(b + 1) * HG * P].rearrange("p (g t) -> p g t", g=HG),
                                   ident_s[:, :].unsqueeze(1).to_broadcast([P, HG, P]),
                                   p0[:, b * HG:(b + 1) * HG].unsqueeze(2).to_broadcast([P, HG, P]),
                                   ALU.mult).then_inc(diag_done[b], 1)

            def x_low(n, p, _):
                pool.wait_ge(xnT_ready, n)
                pool.wait_ge(xh_ready, n)
                pool.tensor_tensor(xl[:, :, :], xnT[:, :, 1:T + 1], xh[:, :, :], ALU.subtract)\
                    .then_inc(xl_ready, 1)

            def o_power(n, p, _, b):
                half = slice(b * HG, (b + 1) * HG)
                pool.wait_ge(ss_eps_ready[b], n)
                wait(pool, on_ready[b], p)
                pool.tensor_tensor(rs[:, half], ss[:, half], minus_half[:, half], ALU.pow)\
                    .then_inc(rs_ready[b], 1)

            def body(A, F, K):
                do(h_low, F, 2)
                do(h_low, F, 3)
                do(mix_sum, F, 0)
                do(h_low, F, 4)
                do(k_step, K, 1)
                do(ln_power, A)
                do(k_step, K, 2)
                do(mix_sum, F, 1)
                do(k_step, K, 3)
                do(mix_sum, F, 2)
                do(k_step, K, 4)
                do(k_step, K, 5)
                do(h_low, F, 5)
                do(k_step, K, 6)
                do(mix_sum, F, 3)
                do(h_low, F, 6)
                do(mix_sum, F, 4)
                do(h_low, F, 7)
                do(o_power, K, 0)
                do(o_power, K, 1)
                do(x_low, A)
                do(h_low, A, 0)
                do(h_low, A, 1)
                do(diagonal_in, F, 0)
                do(diagonal_in, F, 1)
                do(k_step, F, 0)

            rows(pool, body)

        @block.vector
        def _(dve):
            step = [0]

            def then(ins):
                step[0] += 1
                ins.then_inc(su, 1)
                dve.wait_ge(su, step[0])

            dve.wait_ge(const_loaded, 16 * len(loads))
            dve.tensor_copy(masks_s[:, :, :].rearrange("p l t -> p (l t)"), masks_f)
            then(dve.tensor_copy(wx0_h[:, :, :], wx0_f[:, :, :]))
            dve.tensor_tensor(wx0_l[:, :, :], wx0_f[:, :, :], wx0_h[:, :, :], ALU.subtract)
            then(dve.tensor_copy(wx2_s[:, :, :], wx2_f[:, :, :]))
            for q in (1, 3):
                s = slice(R * q, R * q + R)
                dve.tensor_tensor(wx2_s[s, :, :], wx2_f[s, :, :], wx2_s[s, :, :], ALU.subtract)
            then(dve.tensor_copy(ww2_h[:, :], ww2_f[:, :]))
            dve.tensor_tensor(ww2_l[:, :], ww2_f[:, :], ww2_h[:, :], ALU.subtract)
            wv_heads = wv_s[:, :, :].rearrange("p a (h v) -> p (a h) v", v=DV)
            then(dve.tensor_reduce(wv_mean[:, :], wv_heads, AX_X, ALU.add))
            then(dve.tensor_scalar(wv_mean[:, :], wv_mean[:, :], 1.0 / DV, None, ALU.mult))
            dve.tensor_tensor(wv_heads, wv_heads,
                              wv_mean[:, :].unsqueeze(2).to_broadcast([P, HB * NH, DV]), ALU.subtract)
            dve.tensor_scalar(gnw_s[:, :], gnw_s[:, :], 0.5 * DV ** 0.5, None, ALU.mult)
            dve.tensor_scalar(gnb_s[:, :], gnb_s[:, :], 0.5, None, ALU.mult)
            dve.tensor_scalar(b2_s[:, :], b2_s[:, :], 0.5, None, ALU.mult)
            dve.wait_ge(abs_done, 2)
            then(dve.tensor_reduce(alpha1[:, :], w1_rows_s, AX_X, ALU.add))
            dve.tensor_scalar(alpha1[:, :], alpha1[:, :], 1.0 / HID, None, ALU.mult)
            then(dve.tensor_reduce(alpha2[:, :], w2_rows_s, AX_X, ALU.add))
            dve.tensor_scalar(alpha2[:, :], alpha2[:, :], 0.5 / (MT * P), None, ALU.mult)\
                .then_inc(setup_dve, 1)
            dve.wait_ge(setup_dve, 1)
            dve.wait_ge(setup_pool, 1)

            def ln_stats_step(n, p, _):
                dve.wait_ge(x_loaded, 16 * n)
                for c in range(C):
                    last = dve.bn_stats(stats[:, c, :], xt[:, c, :])
                last.then_inc(ln_stats, 1)
                dve.wait_ge(setup_dve, 1)
                dve.wait_ge(ln_stats, n)
                for c in range(C):
                    last = dve.bn_aggr(meanvar[:, c, :], stats[:, c, :])
                last.then_inc(ln_aggr, 1)
                dve.wait_ge(ln_aggr, n)
                wait(dve, ln_rstd, p)
                dve.tensor_scalar(var_eps[:, :], meanvar[:, :, 1], LN_EPS, None, ALU.add)\
                    .then_inc(ln_var, 1)

            def ln_apply(n, p, _):
                dve.wait_ge(ln_rstd, n)
                for c in range(C):
                    last = dve.tensor_scalar(xt[:, c, :], xt[:, c, :], meanvar[:, c, 0:1],
                                             rstd[:, c:c + 1], ALU.subtract, ALU.mult)
                last.then_inc(xn_ready, 1)

            def shift(n, p, _):
                dve.wait_ge(xnT_ready, n)
                dve.tensor_tensor(delta[:, :, :], xnT[:, :, 0:T], xnT[:, :, 1:T + 1], ALU.subtract)\
                    .then_inc(delta_ready, 1)
                dve.wait_ge(delta_ready, n)
                for a in range(HB):
                    last = dve.scalar_tensor_tensor(y0[:, a, :], delta[:, a, :], mu0_s[:, a:a + 1],
                                                    xnT[:, a, 1:T + 1], ALU.mult, ALU.add)
                last.then_inc(y0_ready, 1)

            def y0_low(n, p, _):
                dve.wait_ge(y0h_ready, n)
                dve.wait_ge(y0_ready, n)
                wait(dve, xp_psum, p)
                dve.tensor_tensor(y0l[:, :, :], y0[:, :, :], y0h[:, :, :], ALU.subtract)\
                    .then_inc(y0l_ready, 1)

            def split_xpw(n, p, _):
                dve.wait_ge(xpw_tanh, n)
                dve.wait_ge(xpw_high, n)
                low = slice(2 * R, 4 * R)
                dve.tensor_tensor(xps[low, MW, :], xpt[low, 0, :], xps[low, MW, :], ALU.subtract)\
                    .then_inc(xpw_ready, 1)

            def split_xp(n, p, _):
                dve.wait_ge(xp_tanh, n)
                for k in (MR, MK, MV, MG):
                    wait(dve, xps_loaded[k], 64 * p)
                dve.wait_ge(xph_ready, n)
                dve.tensor_tensor(xpl[:, :], xpt[:, 1, :], xph[:, :], ALU.subtract)\
                    .then_inc(xpl_ready, 1)

            def mix(n, p, _, o):
                k = ORDER[o]
                dve.wait_ge(mus_psum, NMU * p + o + 1)
                wait(dve, y_ready, NMU * p + max(o - 1, 0))
                for a in range(HB):
                    last = dve.scalar_tensor_tensor(yt[:, o % 2, a * T:(a + 1) * T],
                                                    front_ps[:, a * T:(a + 1) * T], xb_s[:, a, k:k + 1],
                                                    delta[:, a, :], ALU.add, ALU.mult)
                last.then_inc(yt_ready, 1)

            def split_w(n, p, _):
                dve.wait_ge(wt_ready, n)
                dve.wait_ge(wsth_ready, n)
                dve.tensor_tensor(wst[GLR:P, :], wt[GLR:P, :], wst[GLR:P, :], ALU.subtract)\
                    .then_inc(wst_ready, 1)

            def g_silu(n, p, _):
                dve.wait_ge(tg_ready, n)
                for b in range(2):
                    wait(dve, og_ready[b], p)
                dve.scalar_tensor_tensor(sg[:, :, :], tg[:, :, :], 1.0,
                                         front_ps[:, :].rearrange("p (a t) -> p a t", a=HB),
                                         ALU.add, ALU.mult).then_inc(sg_ready, 1)

            def z_silu(n, p, _):
                dve.wait_ge(tz_ready, n)
                dve.scalar_tensor_tensor(gate[:, :, :], gate[:, :, :], 1.0, zh[:, :, :],
                                         ALU.add, ALU.mult).then_inc(gate_ready, 1)

            def take(n, p, _):
                dve.wait_ge(r_ready, n)
                dve.wait_ge(k_ready, n)
                wait(dve, Rl_ready, p)
                dve.tensor_copy(Rw[:, :], rkF[:, 0, :])
                wait(dve, kt_psum, p)
                dve.tensor_copy(Kw[:, :], rkF[:, 1, :]).then_inc(rk_taken, 1)
                wait(dve, diag_psum, p)
                dve.scalar_tensor_tensor(zd[:, :], rkF[:, 0, :], u_s[:, 0:1], rkF[:, 1, :],
                                         ALU.mult, ALU.mult).then_inc(zd_ready, 1)

            def decays(n, p, _, levels):
                for l in levels:
                    pair = Dw[l - 1][:, :].rearrange("p (b two) -> p b two", two=2)
                    if l > 1:
                        dve.wait_ge(D_ready, L * p + l - 1)
                    else:
                        dve.wait_ge(d_ready, n)
                        wait(dve, k_upd, L * p)
                    dve.tensor_tensor(Dw[l][:, :], pair[:, :, 0], pair[:, :, 1], ALU.mult)\
                        .then_inc(D_ready, 1)

            def diagonal_out(n, p, _):
                dve.wait_ge(diag_psum, n)
                for b in range(2):
                    wait(dve, diag_done[b], p)
                dve.tensor_copy(p0[:, :], back_ps[:, 0:CH]).then_inc(p0_ready, 1)

            def select(n, p, _, l, b):
                m = 1 << l
                dve.wait_ge(setup_dve, 1)
                if l == 0:
                    dve.wait_ge(diag_done[b], n)
                dve.wait_ge(lev_psum[b], L * p + l + 1)
                dst = PT[:, b * HG * P:(b + 1) * HG * P]\
                    .rearrange("p (g b two m) -> p g b two m", g=HG, two=2, m=m)[:, :, :, 1, :]
                src = back_ps[:, b * BANK:(b + 1) * BANK].rearrange("p (g b m) -> p g b m", g=HG, m=m)
                msk = masks_s[:, l, :].rearrange("p (b m) -> p b m", m=m).unsqueeze(1)\
                    .to_broadcast([P, HG, HALF // m, m])
                dve.copy_predicated(dst, msk, src).then_inc(sel_done[b], 1)

            def r_step(n, p, _, l):
                m = 1 << l
                dve.wait_ge(rx_ready, L * p + l + 1)
                if l:
                    dve.wait_ge(D_ready, L * p + l)
                    dve.wait_ge(r_upd, L * p + l)
                D1 = Dw[l][:, :].rearrange("p (b two) -> p b two", two=2)[:, :, 0:1]\
                    .to_broadcast([P, T // (2 * m), m])
                dve.tensor_tensor(blocks(Rw[:, :], 1, m), blocks(Rw[:, :], 1, m), D1, ALU.mult)\
                    .then_inc(r_upd, 1)

            def split_v(n, p, _):
                dve.wait_ge(vh_ready, n)
                wait(dve, o_psum[1], p)
                dve.tensor_tensor(vl[:, :, :], front_ps[:, :].rearrange("p (c v) -> p c v", c=C),
                                  vh[:, :, :], ALU.subtract).then_inc(vl_ready, 1)

            def split_r(n, p, _):
                dve.wait_ge(r_upd, L * n)
                wait(dve, o_psum[1], p)
                dve.tensor_copy(Rh[:, :], Rw[:, :]).then_inc(Rh_ready, 1)
                dve.wait_ge(Rh_ready, n)
                dve.tensor_tensor(Rl[:, :], Rw[:, :], Rh[:, :], ALU.subtract).then_inc(Rl_ready, 1)

            def split_kt(n, p, _):
                dve.wait_ge(kth_ready, n)
                wait(dve, u_psum, p)
                kt_ps = back_ps[:, BANK:BANK + (C - 1) * P].rearrange("p (c k) -> p c k", c=C - 1)
                dve.tensor_tensor(Ktl[:, :, :], kt_ps, Kth[:, :, :], ALU.subtract)\
                    .then_inc(ktl_ready, 1)

            def scores_low(n, p, _, b):
                dve.wait_ge(ph_ready[b], n)
                half = slice(b * HG * P, (b + 1) * HG * P)
                dve.tensor_tensor(Pl[:, half], PT[:, half], Ph[:, half], ALU.subtract)\
                    .then_inc(pl_ready[b], 1)

            def states(n, p, _):
                dve.wait_ge(u_psum, n)
                wait(dve, sxl_ready, p)
                dve.tensor_copy(St[:, 0, :], back_ps[:, BANK:BANK + DV]).then_inc(st_ready, 1)
                for c in range(1, C - 1):
                    dve.wait_ge(st_ready, (C - 1) * p + c)
                    dve.scalar_tensor_tensor(St[:, c, :], St[:, c - 1, :], Dw[L][:, c:c + 1],
                                             back_ps[:, BANK + c * DV:BANK + (c + 1) * DV], ALU.mult, ALU.add)\
                        .then_inc(st_ready, 1)
                dve.wait_ge(st_ready, (C - 1) * n)
                for h in range(NH):
                    q = slice(DK * h, DK * h + DK)
                    last = dve.tensor_copy(Sxh[q, :, h, :], St[q, :, :])
                last.then_inc(sxh_ready, 1)
                dve.wait_ge(sxh_ready, n)
                for h in range(NH):
                    q = slice(DK * h, DK * h + DK)
                    last = dve.tensor_tensor(Sxl[q, :, h, :], St[q, :, :], Sxh[q, :, h, :],
                                             ALU.subtract)
                last.then_inc(sxl_ready, 1)

            def o_variance(n, p, _, b):
                half = slice(b * HG, (b + 1) * HG)
                dve.wait_ge(osq_ready[b], n)
                dve.tensor_reduce(ss[:, half], on[:, half, :], AX_X, ALU.add).then_inc(ss_ready[b], 1)
                dve.wait_ge(ss_ready[b], n)
                dve.tensor_scalar(ss[:, half], ss[:, half], DV * GN_EPS, None, ALU.add)\
                    .then_inc(ss_eps_ready[b], 1)

            def o_normalise(n, p, _, b):
                half = slice(b * HG, (b + 1) * HG)
                dve.wait_ge(rs_ready[b], n)
                dve.tensor_tensor(on[:, half, :],
                                  back_ps[:, b * BANK:(b + 1) * BANK].rearrange("p (g v) -> p g v", v=DV),
                                  rs[:, half].unsqueeze(2).to_broadcast([P, HG, DV]), ALU.mult)\
                    .then_inc(on_ready[b], 1)

            def o_gate(n, p, _, b):
                tok = slice(b * HT, (b + 1) * HT)
                dve.wait_ge(oT_ready[b], n)
                dve.wait_ge(sg_ready, n)
                dve.tensor_tensor(og[:, :, tok], og[:, :, tok], sg[:, :, tok], ALU.mult)\
                    .then_inc(og_ready[b], 1)

            def s_gate(n, p, _, b):
                tok = slice(b * HT, (b + 1) * HT)
                dve.wait_ge(s_psum[b], n)
                dve.wait_ge(gate_ready, n)
                wait(dve, outT_psum[b], p)
                dve.tensor_tensor(sgt[:, :, tok],
                                  back_ps[:, b * BANK:(b + 1) * BANK].rearrange("p (a t) -> p a t", a=HB),
                                  gate[:, :, tok], ALU.mult).then_inc(sgt_ready[b], 1)

            def residual(n, p, _, b):
                chunks = slice(b * HC, (b + 1) * HC)
                dve.wait_ge(outT_psum[b], n)
                dve.wait_ge(xres_loaded, 16 * n)
                dve.tensor_tensor(xres[:, chunks, :],
                                  back_ps[:, b * BANK:(b + 1) * BANK].rearrange("p (c h) -> p c h", c=HC),
                                  xres[:, chunks, :], ALU.add).then_inc(out_ready[b], 1)

            def body(A, F, K):
                do(ln_stats_step, A)
                do(r_step, K, 2)
                do(select, K, 2, 0)
                do(split_w, F)
                do(r_step, K, 3)
                do(select, K, 2, 1)
                do(mix, F, 2)
                do(r_step, K, 4)
                do(select, K, 3, 0)
                do(select, K, 3, 1)
                do(ln_apply, A)
                do(z_silu, K)
                do(select, K, 4, 0)
                do(select, K, 4, 1)
                do(r_step, K, 5)
                do(mix, F, 3)
                do(select, K, 5, 0)
                do(r_step, K, 6)
                do(select, K, 5, 1)
                do(split_r, K)
                do(select, K, 6, 0)
                do(select, K, 6, 1)
                do(mix, F, 4)
                do(split_kt, K)
                do(scores_low, K, 0)
                do(states, K)
                do(scores_low, K, 1)
                do(shift, A)
                do(o_variance, K, 0)
                do(split_v, F)
                do(o_variance, K, 1)
                do(take, F)
                do(o_normalise, K, 1)
                do(o_normalise, K, 0)
                do(y0_low, A)
                do(o_gate, K, 1)
                do(o_gate, K, 0)
                do(g_silu, F)
                do(s_gate, K, 1)
                do(s_gate, K, 0)
                do(residual, K, 0)
                do(diagonal_out, F)
                do(split_xp, A)
                do(residual, K, 1)
                do(r_step, F, 0)
                do(decays, F, range(1, 4))
                do(split_xpw, A)
                do(select, F, 0, 0)
                do(select, F, 0, 1)
                do(decays, F, range(4, L + 1))
                do(r_step, F, 1)
                do(mix, A, 0)
                do(select, F, 1, 0)
                do(mix, A, 1)
                do(select, F, 1, 1)

            rows(dve, body)

        @block.tensor
        def _(pe):
            pe.wait_ge(setup_dve, 1)
            pe.wait_ge(setup_pool, 1)
            pe.wait_ge(sign_done, 1)

            def mm(dst, pairs, start=True, stop=True):
                for k, (a, b) in enumerate(pairs):
                    last = pe.matmul(dst, a, b, start=start and k == 0, stop=stop and k == len(pairs) - 1,
                                     skip_group_check=True)
                return last

            def x_transpose(n, p, _):
                pe.wait_ge(xn_ready, n)
                wait(pe, gelu_done, MT * p)
                for c in range(C):
                    for a in range(HB):
                        last = pe.transpose(hid_ps[:, a, c * P:(c + 1) * P],
                                            xt[:, c, a * P:(a + 1) * P], ident_s[:, :])
                last.then_inc(xnT_psum, 1)

            def mix_rank(n, p, _):
                pe.wait_ge(y0l_ready, n)
                wait(pe, sg_ready, p)
                for k, done in ((0, xpw_psum), (1, xp_psum)):
                    cols = slice(k * P, (k + 1) * P)
                    mm(front_ps[:, k * T:(k + 1) * T],
                       [(w[:, a, cols], y[:, a, :]) for a in range(HB)
                        for w, y in ((wx0_h, y0h), (wx0_l, y0h), (wx0_h, y0l))]).then_inc(done, 1)

            def ffn1(n, p, _, m):
                if m == 0:
                    pe.wait_ge(xh_ready, n)
                    pe.wait_ge(xl_ready, n)
                wait(pe, gelu_done, MT * p + max(m - 1, 0))
                mm(hid_ps[:, m % 2, :], [(sign1[:, a, m * P:(m + 1) * P], part[:, a, :])
                                         for a in range(HB) for part in (xh, xl)]).then_inc(hid_psum, 1)

            def ffn2(n, p, _, m):
                if m == 0:
                    wait(pe, zh_ready, p)
                pe.wait_ge(hl_ready, MT * p + m + 1)
                for a in range(HB):
                    last = mm(ffn_ps[:, a, :], [(sign2[:, m, a * P:(a + 1) * P], part[:, m % 2, :])
                                                for part in (hh, hl)], start=m == 0, stop=m == MT - 1)
                last.then_inc(ffn2_done, 1)

            def mus(n, p, _, o):
                k = ORDER[o]
                if o == 0:
                    pe.wait_ge(xpw_ready, n)
                    pe.wait_ge(xp_tanh, n)
                else:
                    pe.wait_ge(xps_loaded[k], 64 * n)
                if o == 1:
                    pe.wait_ge(yt_ready, NMU * p + 1)
                if o == 2:
                    pe.wait_ge(wt_ready, n)
                    pe.wait_ge(yt_ready, NMU * p + 2)
                if o == 3:
                    pe.wait_ge(ew_ready, n)
                    pe.wait_ge(r_ready, n)
                if o == 4:
                    pe.wait_ge(k_ready, n)
                for a in range(HB):
                    last = mm(front_ps[:, a * T:(a + 1) * T], [(wx2_s[:, k, a * P:(a + 1) * P], xps[:, k, :])])
                last.then_inc(mus_psum, 1)

            def project(dst, w, o):
                return mm(dst, [(w[:, a, :], yy[:, o % 2, a * T:(a + 1) * T]) for a in range(HB)])

            def w_rank(n, p, _):
                pe.wait_ge(yt_ready, NMU * p + 2)
                pe.wait_ge(y_ready, NMU * p + 1)
                project(front_ps[:, 0:T], ww1_s, 0).then_inc(w1_psum, 1)

            def w_proj(n, p, _):
                pe.wait_ge(yt_ready, NMU * p + 3)
                pe.wait_ge(wst_ready, n)
                mm(front_ps[:, 0:T], [(ww2_h[:, :], wst[:, :]), (ww2_l[:, :], wst[:, :])])\
                    .then_inc(w2_psum, 1)

            def r_proj(n, p, _):
                pe.wait_ge(y_ready, NMU * p + 2)
                project(front_ps[:, T:2 * T], wr_s, 1).then_inc(r_psum, 1)

            def k_proj(n, p, _):
                pe.wait_ge(yt_ready, NMU * p + 4)
                pe.wait_ge(y_ready, NMU * p + 3)
                project(front_ps[:, 0:T], wk_s, 2).then_inc(k_psum, 1)

            def v_proj(n, p, _):
                pe.wait_ge(yt_ready, NMU * p + 5)
                pe.wait_ge(y_ready, NMU * p + 4)
                for c in range(C):
                    last = mm(front_ps[:, c * VD:(c + 1) * VD],
                              [(yy[:, 1, a * T + c * P:a * T + (c + 1) * P], wv_s[:, a, :])
                               for a in range(HB)])
                last.then_inc(v_psum, 1)

            def g_proj(n, p, _):
                pe.wait_ge(vl_ready, n)
                pe.wait_ge(y_ready, NMU * p + 5)
                for a in range(HB):
                    last = project(front_ps[:, a * T:(a + 1) * T], wg_s[:, :, a * P:(a + 1) * P], 4)
                last.then_inc(g_psum, 1)

            def diagonal(n, p, _):
                pe.wait_ge(zd_ready, n)
                wait(pe, out_ready[0], p)
                for c in range(C):
                    last = mm(back_ps[:, c * NH:(c + 1) * NH], [(zd[:, c * P:(c + 1) * P], ones_s[:, :])])
                last.then_inc(diag_psum, 1)

            def level(n, p, _, l, b):
                pe.wait_ge(rx_ready, L * p + l + 1)
                if l:
                    pe.wait_ge(k_upd, L * p + l)
                    pe.wait_ge(sel_done[b], L * p + l)
                else:
                    pe.wait_ge(rk_taken, n)
                    pe.wait_ge(p0_ready, n)
                    wait(pe, out_ready[b], p)
                for c in range(b * HC, (b + 1) * HC):
                    last = mm(back_ps[:, c * NH * HALF:(c + 1) * NH * HALF],
                              [(Kw[:, c * P:(c + 1) * P],
                                Rx[:, l % 2, c * NH * HALF:(c + 1) * NH * HALF])])
                last.then_inc(lev_psum[b], 1)

            def k_transpose(n, p, _):
                pe.wait_ge(k_upd, L * n)
                pe.wait_ge(sel_done[1], L * n)
                for c in range(C - 1):
                    last = pe.transpose(back_ps[:, BANK + c * P:BANK + (c + 1) * P],
                                        Kw[:, c * P:(c + 1) * P], ident_s[:, :])
                last.then_inc(kt_psum, 1)

            def updates(n, p, _):
                pe.wait_ge(ktl_ready, n)
                pe.wait_ge(vl_ready, n)
                for c in range(C - 1):
                    for h in range(NH):
                        kq = slice(DK * h, DK * h + DK)
                        vq = slice(DV * h, DV * h + DV)
                        last = mm(back_ps[kq, BANK + c * DV:BANK + (c + 1) * DV],
                                  [(Kth[:, c, kq], vh[:, c, vq]), (Kth[:, c, kq], vl[:, c, vq]),
                                   (Ktl[:, c, kq], vh[:, c, vq])])
                last.then_inc(u_psum, 1)

            def attend(n, p, _, b):
                pe.wait_ge(sxl_ready, n)
                pe.wait_ge(Rl_ready, n)
                pe.wait_ge(ph_ready[b], n)
                pe.wait_ge(pl_ready[b], n)
                for c in range(b * HC, (b + 1) * HC):
                    tok = slice(c * P, (c + 1) * P)
                    if c:
                        sh = Sxh[:, c - 1, :, :].rearrange("p h v -> p (h v)")
                        sl = Sxl[:, c - 1, :, :].rearrange("p h v -> p (h v)")
                        mm(back_ps[:, c * VD:(c + 1) * VD],
                           [(Rh[:, tok], sh), (Rh[:, tok], sl), (Rl[:, tok], sh)], stop=False)
                    for h in range(NH):
                        g = slice((c * NH + h) * P, (c * NH + h + 1) * P)
                        vq = slice(DV * h, DV * h + DV)
                        last = mm(back_ps[:, c * VD + DV * h:c * VD + DV * h + DV],
                                  [(Ph[:, g], vh[:, c, vq]), (Ph[:, g], vl[:, c, vq]),
                                   (Pl[:, g], vh[:, c, vq])], start=c == 0, stop=True)
                last.then_inc(o_psum[b], 1)

            def o_transpose(n, p, _, b):
                pe.wait_ge(on_ready[b], n)
                onf = on[:, :, :].rearrange("p (c h) v -> p c (h v)", c=C)
                for c in range(HC):
                    for a in range(HB):
                        col = b * BANK + a * HT + c * P
                        last = pe.transpose(back_ps[:, col:col + P],
                                            onf[:, b * HC + c, a * P:(a + 1) * P], ident_s[:, :])
                last.then_inc(oT_psum[b], 1)

            def o_proj(n, p, _, b):
                pe.wait_ge(og_ready[b], n)
                for m in range(HB):
                    last = mm(back_ps[:, b * BANK + m * HT:b * BANK + (m + 1) * HT],
                              [(wo_s[:, a, m * P:(m + 1) * P], og[:, a, b * HT:(b + 1) * HT])
                               for a in range(HB)])
                last.then_inc(s_psum[b], 1)

            def s_transpose(n, p, _, b):
                pe.wait_ge(sgt_ready[b], n)
                for c in range(b * HC, (b + 1) * HC):
                    for a in range(HB):
                        last = pe.transpose(back_ps[:, c * HID + a * P:c * HID + (a + 1) * P],
                                            sgt[:, a, c * P:(c + 1) * P], ident_s[:, :])
                last.then_inc(outT_psum[b], 1)

            def body(A, F, K):
                do(mus, F, 1)
                do(level, K, 1, 1)
                do(ffn2, F, 3)
                do(w_rank, F)
                do(level, K, 2, 0)
                do(level, K, 2, 1)
                do(mus, F, 2)
                do(ffn1, F, 6)
                do(level, K, 3, 0)
                do(level, K, 3, 1)
                do(w_proj, F)
                do(r_proj, F)
                do(level, K, 4, 0)
                do(level, K, 4, 1)
                do(ffn2, F, 4)
                do(mus, F, 3)
                do(level, K, 5, 0)
                do(level, K, 5, 1)
                do(k_proj, F)
                do(level, K, 6, 0)
                do(level, K, 6, 1)
                do(mus, F, 4)
                do(ffn1, F, 7)
                do(k_transpose, K)
                do(ffn2, F, 5)
                do(updates, K)
                do(x_transpose, A)
                do(v_proj, F)
                do(attend, K, 0)
                do(attend, K, 1)
                do(ffn2, F, 6)
                do(ffn2, F, 7)
                do(g_proj, F)
                do(o_transpose, K, 1)
                do(o_transpose, K, 0)
                do(ffn1, A, 0)
                do(o_proj, K, 1)
                do(o_proj, K, 0)
                do(ffn1, A, 1)
                do(s_transpose, K, 1)
                do(s_transpose, K, 0)
                do(mix_rank, A)
                do(ffn1, A, 2)
                do(diagonal, F)
                do(ffn2, A, 0)
                do(ffn1, A, 3)
                do(level, F, 0, 0)
                do(level, F, 0, 1)
                do(ffn2, A, 1)
                do(mus, A, 0)
                do(ffn1, A, 4)
                do(level, F, 1, 0)
                do(ffn1, A, 5)
                do(ffn2, A, 2)

            rows(pe, body)


def _layouts(np, a):
    P_ = 128
    T_, R_, NH_, L_ = 512, 32, 4, 7
    HID_ = a["L0_attn_W_r"].shape[1]

    def cols(v):
        return v.reshape(-1, P_).T

    def lhsT(w):
        return w.T.reshape(-1, P_, w.shape[0]).transpose(1, 0, 2)

    t = np.arange(P_)
    masks = np.zeros((P_, L_, P_ // 2), np.float32)
    for l in range(L_):
        m = 1 << l
        k = np.arange(P_ // 2)
        masks[:, l, :] = (t[:, None] // (2 * m) == k[None, :] // m) & (t[:, None] % (2 * m) < m)
    return {
        "x": a["L0_attn_hidden_states"],
        "mu0": cols(a["L0_attn_mu0"]),
        "wx0": lhsT(a["L0_attn_W_x0"].reshape(5, R_, HID_)[[1, 1, 1, 1, 0, 2, 3, 4]].reshape(-1, HID_)),
        "wx2": np.tile(a["L0_attn_W_x2"].reshape(HID_, 5, R_).transpose(2, 1, 0), (4, 1, 1)),
        "x_bias": a["L0_attn_x_bias"].reshape(5, -1, P_).transpose(2, 1, 0),
        "wr": lhsT(a["L0_attn_W_r"]),
        "ww1": np.tile(lhsT(a["L0_attn_W_w1"]), (1, 1, 2)),
        "ww2": np.tile(a["L0_attn_W_w2"].T, (2, 1)),
        "b_w2": cols(a["L0_attn_b_w2"]),
        "wk": lhsT(a["L0_attn_W_k"]),
        "wv": lhsT(a["L0_attn_W_v"]),
        "wg": lhsT(a["L0_attn_W_g"]),
        "bonus": a["L0_attn_bonus"].reshape(P_, 1),
        "gn_w": cols(a["L0_attn_gn_weight"]),
        "gn_b": cols(a["L0_attn_gn_bias"]),
        "wo": lhsT(a["L0_attn_W_o"]),
        "w1_rows": a["L0_ffn_w1"].reshape(-1, P_, HID_).transpose(1, 0, 2),
        "w1_cols": lhsT(a["L0_ffn_w1"]).reshape(P_, -1),
        "b1": cols(a["L0_ffn_b1"]),
        "w2_rows": a["L0_ffn_w2"].reshape(-1, P_, a["L0_ffn_w2"].shape[1]).transpose(1, 0, 2),
        "w2_cols": lhsT(a["L0_ffn_w2"]).reshape(P_, -1),
        "b2": cols(a["L0_ffn_b2"]),
        "ident": np.eye(P_, dtype=np.float32),
        "level_masks": masks.reshape(P_, -1),
        "head_ones": (t[:, None] // (P_ // NH_) == np.arange(NH_)[None, :]).astype(np.float32),
    }


def kernel(**inputs):
    import numpy as np
    import concourse.bacc as bacc
    from concourse.bass_utils import run_bass_kernel_spmd

    arrays = {k: np.asarray(v) for k, v in inputs.items()}
    laid = {k: np.ascontiguousarray(v) for k, v in _layouts(np, arrays).items()}
    nc = bacc.Bacc("TRN2", target_bir_lowering=False, num_devices=1)
    args, feed = {}, {}
    for name, a in laid.items():
        feed[f"in_{name}"] = a
        args[name] = nc.dram_tensor(f"in_{name}", a.shape, mybir.dt.from_np(a.dtype), kind="ExternalInput").ap()
    y = nc.dram_tensor("out_y", laid["x"].shape, F32, kind="ExternalOutput").ap()
    rwkv6_gated_ffn(nc, out=y, **args)
    r = run_bass_kernel_spmd(nc, [feed], core_ids=[0])
    return r.results[0]["out_y"]
```
